# Optimizing a Trainium2 kernel written in Bass

```python
import numpy as np
import jax
import jax.numpy as jnp

def _softmax(x, axis=-1):
    return jax.nn.softmax(x, axis=axis)

def _gelu(x):
    return jax.nn.gelu(x, approximate=True)

def _silu(x):
    return jax.nn.silu(x)

def _sigmoid(x):
    return jax.nn.sigmoid(x)

def _layernorm(x, axis=-1, eps=1e-05):
    m = jnp.mean(x, axis=axis, keepdims=True)
    v = jnp.var(x, axis=axis, keepdims=True)
    return (x - m) / jnp.sqrt(v + eps)

def _scatter_add(tgt, idx, src, axis=0):
    return tgt.at[idx].add(src)

def _segment_sum(src, seg, n):
    return jax.ops.segment_sum(src, seg, n)
kernel_name = 'mk_adj_ffn_d1_adj_r2_63a4e3'

def setup_inputs(seed: int=0):
    np.random.seed(seed)
    _w = jnp.asarray

    def _rec_inputs():
        import jax
        import jax.numpy as jnp
        _gk = jax.random.key(seed)
        x = -0.000929 + 1 * jax.random.normal(jax.random.fold_in(_gk, 1), (16, 512, 256), jnp.float32)
        _w = (1.0 + jnp.arange(512, dtype=jnp.float32)) ** (-0.5)
        _w = _w / _w.mean()
        _pij = jnp.clip(0.0078125 * _w[:, None] * _w[None, :], 0.0, 1.0)
        _a = jax.random.uniform(jax.random.fold_in(_gk, 2), (512, 512)) < _pij
        adj = _a.astype(jnp.int32)
        return (x, adj)
    x, adj = _rec_inputs()

    def _L0_gnn_setup():
        import jax, jax.numpy as jnp
        import numpy as np
        B, K, DIN, DOUT = (32, 64, 256, 256)
        key = jax.random.key(seed)
        k1, k2, k3, k4 = jax.random.split(key, 4)
        x = jax.random.normal(k1, (B, K, DIN), dtype=jnp.float32)
        adj = jax.random.randint(k2, (K, K), 0, 2, dtype=jnp.int32)
        W = jax.random.normal(k3, (DOUT, 2 * DIN), dtype=jnp.float32) * 0.02
        b = jax.random.normal(k4, (DOUT,), dtype=jnp.float32) * 0.02
        return {'x': x, 'adj': adj, 'W': W, 'b': b}
    _L0_gnn_all = _L0_gnn_setup()
    _L0_gnn_in = {k: v for k, v in _L0_gnn_all.items() if k in ('W', 'b')}
    del _L0_gnn_all

    def _L0_ffn_setup():
        import jax, jax.numpy as jnp
        import numpy as np
        B, N, D, E = (8, 4096, 256, 8)
        H = 2 * D
        key = jax.random.key(seed)
        ks = jax.random.split(key, 7)
        s = 0.02
        return {'x': jax.random.normal(ks[0], (B, N, D), dtype=jnp.float32), 'W1': jax.random.normal(ks[1], (E, D, H), dtype=jnp.float32) * s, 'b1': jnp.zeros((E, H), dtype=jnp.float32), 'W2': jax.random.normal(ks[2], (E, H, D), dtype=jnp.float32) * s, 'b2': jnp.zeros((E, D), dtype=jnp.float32), 'Wg': jax.random.normal(ks[3], (D, E), dtype=jnp.float32) * s, 'bg': jnp.zeros((E,), dtype=jnp.float32)}
    _L0_ffn_all = _L0_ffn_setup()
    _L0_ffn_in = {k: v for k, v in _L0_ffn_all.items() if k in ('W1', 'b1', 'W2', 'b2', 'Wg', 'bg')}
    del _L0_ffn_all
    return {'x': x, 'adj': adj, 'L0_gnn_W': _L0_gnn_in['W'], 'L0_gnn_b': _L0_gnn_in['b'], 'L0_ffn_W1': _L0_ffn_in['W1'], 'L0_ffn_b1': _L0_ffn_in['b1'], 'L0_ffn_W2': _L0_ffn_in['W2'], 'L0_ffn_b2': _L0_ffn_in['b2'], 'L0_ffn_Wg': _L0_ffn_in['Wg'], 'L0_ffn_bg': _L0_ffn_in['bg']}

def reference(x, adj, L0_gnn_W, L0_gnn_b, L0_ffn_W1, L0_ffn_b1, L0_ffn_W2, L0_ffn_b2, L0_ffn_Wg, L0_ffn_bg):
    import jax
    import jax.numpy as jnp

    def _L0_gnn_ref(x, adj, W, b):
        import jax, jax.numpy as jnp
        import numpy as np
        B, K, DIN, DOUT = (32, 64, 256, 256)
        Din = x.shape[-1]
        Wi, Wj = (W[:, :Din], W[:, Din:])
        mi = jnp.einsum('bkd,od->bko', x, Wi)
        mj = jnp.einsum('bkd,od->bko', x, Wj)
        a = adj.astype(x.dtype)
        deg = a.sum(axis=1)
        out = deg[None, :, None] * (mi + b) + jnp.einsum('ij,bjo->bio', a, mj)
        return out

    def _L0_ffn_ref(x, W1, b1, W2, b2, Wg, bg):
        import jax, jax.numpy as jnp
        import numpy as np
        B, N, D, E = (8, 4096, 256, 8)
        H = 2 * D
        Bs, Ns, Ds = x.shape
        xf = x.reshape(Bs * Ns, Ds)
        logits = xf @ Wg + bg
        idx = jnp.argmax(logits, axis=-1)
        out = jnp.zeros_like(xf)
        num_experts = W1.shape[0]
        for e in range(num_experts):
            h = jax.nn.relu(xf @ W1[e] + b1[e])
            y = h @ W2[e] + b2[e]
            out = jnp.where((idx == e)[:, None], y, out)
        return out.reshape(Bs, Ns, Ds)
    x = x + _L0_gnn_ref(_layernorm(x, axis=-1), adj, L0_gnn_W, L0_gnn_b)
    x = x + _L0_ffn_ref(_layernorm(x, axis=-1), L0_ffn_W1, L0_ffn_b1, L0_ffn_W2, L0_ffn_b2, L0_ffn_Wg, L0_ffn_bg)
    return x

_drawn_inputs = setup_inputs


def setup_inputs(seed=0):
    import zlib

    import numpy as np

    out = dict(_drawn_inputs(seed))
    spreads = {'L0_ffn_b1': (0.0, 0.565), 'L0_ffn_b2': (0.0, 0.1), 'L0_ffn_bg': (0.0, 0.1)}
    factors = {}
    for name, (base, spread) in spreads.items():
        noise = np.random.default_rng([zlib.crc32(name.encode()), seed]).standard_normal(out[name].shape)
        drawn = base * np.exp(spread * noise) if base else spread * noise
        out[name] = jnp.asarray(drawn.astype(out[name].dtype))
    for name, factor in factors.items():
        out[name] = (out[name] * factor).astype(out[name].dtype)
    return out
```

```python
from contextlib import ExitStack

import concourse.bass as bass
from concourse import mybir

F32 = mybir.dt.float32
F32R = mybir.dt.float32r
BF16 = mybir.dt.bfloat16
I32 = mybir.dt.int32
U32 = mybir.dt.uint32
ALU = mybir.AluOpType
ACT = mybir.ActivationFunctionType
AX_X = mybir.AxisListType.X

P = 128
EPS = 1e-5
PAD = 4
TILE = 256
RING = 4
NO_TOKEN = 1 << 20
EXACT = 4096.0


def moe_gnn_kernel(nc, x, adj, gnn_w, gnn_b, w1, b1, w2, b2, wg, bg, out):
    B, S, D = x.shape
    E, _, H = w1.shape
    T = B * S
    NT = S // P
    KD = D // P
    KH = H // P
    TH = TILE // P
    CAP = T + TILE
    ROW = D + PAD
    HALF = NT // 2
    W1N, W2N = KD * H, KH * D
    assert S == 512 and KD == 2 and KH == 4 and NT == 4 and B % 2 == 0 and B >= 8

    rows = nc.dram_tensor("expert_rows", (E * CAP, ROW), F32, kind="Internal").ap()
    out_rows = out.rearrange("b s d -> (b s) d")

    with ExitStack() as ctx:
        def sb(name, shape, dt=F32):
            return ctx.enter_context(nc.sbuf_tensor(name, shape, dt))

        def ps(name, shape):
            return ctx.enter_context(nc.psum_tensor(name, shape, F32))

        def sem(name):
            return ctx.enter_context(nc.semaphore(name))

        agg_ps = [ps(f"agg_ps{d}", [P, 2, S]) for d in range(KD)]
        fin_ps = ps("fin_ps", [P, NT, D])
        tr_ps = ps("tr_ps", [P, S])
        misc_ps = ps("misc_ps", [P, S])
        h_ps = [agg_ps[0][:, 0, 0:TILE], agg_ps[0][:, 1, 0:TILE], agg_ps[1][:, 0, 0:TILE], agg_ps[1][:, 1, 0:TILE]]
        y_ps = [fin_ps[:, 0, :], fin_ps[:, 2, :]]
        th_ps, tl_ps = tr_ps, misc_ps
        logit_ps = misc_ps[:, 0:NT * E]
        rank_ps = misc_ps[:, 64:64 + NT * E]
        total_ps = misc_ps[:, 128:128 + E]
        b1t_ps = tr_ps[:, 0:E * KH]
        big_ps = misc_ps[0:1, 256:257]

        ident = sb("ident", [P, P])
        ident_r = sb("ident_r", [P, P], F32R)
        ones_b = sb("ones_b", [P, P], BF16)
        before_b = sb("before_b", [P, P], BF16)
        ones_f = sb("ones_f", [P, 1])
        minus_half = sb("minus_half", [P, NT])
        token_no = sb("token_no", [P, T // P], I32)
        region = sb("region", [P, NT, E])
        region_i = sb("region_i", [P, NT, E], I32)
        order = sb("order", [P, NT, E])
        order_i = sb("order_i", [P, NT, E], I32)
        filling = sb("filling", [P, TH, ROW])
        adj_h = sb("adj_h", [P, NT, S], F32R)
        adj_l = sb("adj_l", [P, NT, S], F32R)
        deg = sb("deg", [P, NT])
        deg_f = sb("deg_f", [P, NT, P])
        deg_h = sb("deg_h", [P, NT, P], F32R)
        deg_l = sb("deg_l", [P, NT, P], F32R)
        deg_b = sb("deg_b", [P, NT, D])
        gw_h = sb("gw_h", [P, 2 * KD, D], F32R)
        gw_l = sb("gw_l", [P, 2 * KD, D], F32R)
        gb = sb("gb", [P, D])
        wg_sb = sb("wg_sb", [P, KD, E])
        bg_sb = sb("bg_sb", [P, E])
        b1_n = sb("b1_n", [E * KH, P])
        b1_t = sb("b1_t", [P, E * KH])
        b2_sb = sb("b2_sb", [P, E * D])
        big = sb("big", [P, 8])
        big_i = sb("big_i", [1, 1], I32)
        table_f = sb("table_f", [P, 4, E])
        table_i = sb("table_i", [P, 4, E], I32)
        stage = sb("stage", [P, 2, W1N + W2N])
        adj_i = stage[:, 0, :].bitcast(I32).rearrange("p (t s) -> p t s", t=NT)
        adj_f = stage[:, 1, :].rearrange("p (t s) -> p t s", t=NT)
        gw_n = sb("gw_n", [P, KD, 2 * D])

        xin = [sb(f"xin{i}", [P, NT, D]) for i in range(2)]
        xb = [sb(f"xb{i}", [P, NT, D]) for i in range(2)]
        xn = sb("xn", [P, NT, D])
        xn_h = [sb(f"xn_h{i}", [P, NT, D], F32R) for i in range(2)]
        xn_l = [sb(f"xn_l{i}", [P, NT, D], F32R) for i in range(2)]
        split = sb("split", [P, 2, 2, 2 * KD * S], F32R)
        ag = [[split[:, i, hl, :].rearrange("p (d w s) -> p d w s", d=KD, w=2) for hl in range(2)] for i in range(2)]
        x1 = [sb(f"x1_{i}", [P, NT, ROW]) for i in range(2)]
        xm = sb("xm", [P, NT, D])
        xm_h = sb("xm_h", [P, NT, D], F32R)
        xm_l = sb("xm_l", [P, NT, D], F32R)
        xm_t = sb("xm_t", [P, 2, S])
        st1 = sb("st1", [P, NT, 6])
        mv1 = sb("mv1", [P, NT, 2])
        ve1 = sb("ve1", [P, NT])
        nm1 = sb("nm1", [P, NT])
        rs1 = sb("rs1", [P, NT])
        sh1 = sb("sh1", [P, NT])
        st2 = sb("st2", [P, NT, 6])
        mv2 = sb("mv2", [P, NT, 2])
        ve2 = sb("ve2", [P, NT])
        nm2 = sb("nm2", [P, NT])
        rs2 = sb("rs2", [P, NT])
        sh2 = sb("sh2", [P, NT])
        logit = sb("logit", [P, NT, E])
        top = sb("top", [P, NT])
        score = sb("score", [P, NT, E])
        best = sb("best", [P, NT])
        chosen = [sb(f"chosen{i}", [P, NT, E], BF16) for i in range(2)]
        seen = [sb(f"seen{i}", [P, E], BF16) for i in range(2)]
        added = sb("added", [P, E])
        place = sb("place", [P, NT, E])
        slot = sb("slot", [P, NT])
        slot_i = [sb(f"slot_i{i}", [P, NT], I32) for i in range(2)]

        rt = sb("rt", [P, RING, TH, ROW])
        zn = sb("zn", [P, TH, D])
        zn_h = sb("zn_h", [P, TH, D], F32R)
        zn_l = sb("zn_l", [P, TH, D], F32R)
        zt_h = sb("zt_h", [P, KD, TILE], F32R)
        zt_l = sb("zt_l", [P, KD, TILE], F32R)
        hr = sb("hr", [P, KH, TILE])
        hh = sb("hh", [P, KH, TILE], F32R)
        hl_ = sb("hl_", [P, KH, TILE], F32R)
        res = sb("res", [P, TH, D])
        y = sb("y", [P, TH, D])
        tok_early = sb("tok_early", [P, TH], I32)
        tok = sb("tok", [P, TH], I32)
        st3 = sb("st3", [P, TH, 6])
        mv3 = sb("mv3", [P, TH, 2])
        ve3 = sb("ve3", [P, TH])
        nm3 = sb("nm3", [P, TH])
        rs3 = sb("rs3", [P, TH])
        sh3 = sb("sh3", [P, TH])
        ew_h = [split[:, i, 0, :] for i in range(2)]
        ew_l = [split[:, i, 1, :] for i in range(2)]
        w1_h = [w[:, 0:W1N].rearrange("p (k n) -> p k n", k=KD) for w in ew_h]
        w1_l = [w[:, 0:W1N].rearrange("p (k n) -> p k n", k=KD) for w in ew_l]
        w2_h = [w[:, W1N:].rearrange("p (k n) -> p k n", k=KH) for w in ew_h]
        w2_l = [w[:, W1N:].rearrange("p (k n) -> p k n", k=KH) for w in ew_l]

        s_adj = sem("adj_loaded")
        s_gw = sem("gnn_weights_loaded")
        s_small = sem("small_inputs_loaded")
        s_zero = sem("tiles_set")
        s_ident = sem("identity_written")
        s_ones = sem("ones_written")
        s_half = sem("minus_half_written")
        s_const = sem("constants_written")
        CONSTS = 8
        SMALL = 6
        s_ident_r = sem("ident_r_written")
        s_adjf = sem("adjacency_in_float")
        s_adjt = sem("adjacency_transposed")
        s_adjh = sem("adjacency_high")
        s_adjl = sem("adjacency_low")
        s_gwt = sem("gnn_weights_transposed")
        s_gwh = sem("gnn_weights_high")
        s_gwl = sem("gnn_weights_low")
        s_degf = sem("degree_diagonals")
        s_degh = sem("degree_high")
        s_degl = sem("degree_low")
        s_degb = sem("degree_bias")
        s_big = sem("largest_entry")
        s_bigp = sem("large_entries_counted")
        s_bigi = sem("large_entries_flag")
        s_b1t = sem("b1_transposed")
        s_b1 = sem("b1_columns")
        s_x = [sem(f"x_loaded{i}") for i in range(2)]
        s_bn1, s_mv1, s_ve1 = sem("bn1"), sem("mean_var1"), sem("eps_and_minus_mean1")
        s_rs1, s_sh1 = sem("inverse_std1"), sem("shift1")
        s_xn = sem("xn_written")
        s_xnh, s_xnl = sem("xn_high"), sem("xn_low")
        s_xb = sem("xb_written")
        s_agg = sem("aggregated")
        s_agh, s_agl = sem("aggregated_high"), sem("aggregated_low")
        s_fin = sem("weight_products")
        s_x1 = sem("x1_written")
        s_no = sem("token_numbers_in_x1")
        s_bn2, s_mv2, s_ve2 = sem("bn2"), sem("mean_var2"), sem("eps_and_minus_mean2")
        s_rs2, s_sh2 = sem("inverse_std2"), sem("shift2")
        s_xm = sem("xm_written")
        s_xmh, s_xml = sem("xm_high"), sem("xm_low")
        s_tr = sem("xm_transposed")
        s_xmt = sem("xm_transposed_copied")
        s_log = sem("logits")
        s_gate = sem("gate_steps")
        s_seen = sem("seen_updated")
        s_rank = sem("ranks")
        s_slot = sem("slot_steps")
        s_sc = [sem(f"rows_scattered{i}") for i in range(2)]
        s_total = sem("totals")
        s_table = sem("table_steps")
        TABLE = 6
        s_base = sem("tiles_before_steps")
        s_fill = sem("filling_stored")
        s_raw = [sem(f"expert_weights_loaded{i}") for i in range(2)]
        s_ewh, s_ewl = sem("expert_weights_high"), sem("expert_weights_low")
        s_rt = sem("row_tile_loaded")
        s_bn3, s_mv3, s_ve3 = sem("bn3"), sem("mean_var3"), sem("eps_and_minus_mean3")
        s_rs3, s_sh3 = sem("inverse_std3"), sem("shift3")
        s_zn, s_znh, s_znl = sem("zn_written"), sem("zn_high"), sem("zn_low")
        s_zt = sem("zn_transposed")
        s_zth, s_ztl = sem("zn_transposed_high"), sem("zn_transposed_low")
        s_h = sem("hidden_chunks")
        s_hr, s_hh = sem("relu_chunks"), sem("hidden_high")
        s_hl01, s_hl23 = sem("hidden_low_01"), sem("hidden_low_23")
        s_free = sem("ring_tiles_read")
        s_tok = sem("tokens_copied")
        s_yp = sem("output_products")
        s_y = sem("y_written")
        s_out = sem("output_scattered")

        s_passed = sem("waits_passed")

        def hold(engine):
            engine.sem_inc(s_passed, 1)

        def flat(a):
            return a.rearrange("p t e -> p (t e)")

        def nth_of_parity(b, parity, amount):
            return (b - parity) * (amount // 2) + amount

        def reused(b):
            return not isinstance(b, int) or b >= 2

        def later(b):
            return not isinstance(b, int) or b >= 1

        def stages(step, engine, start=-1):
            first, last = 5, B - 1
            for s in range(start, first):
                step(s, s % 2, lambda off, s=s: 0 <= s + off < B)
            with engine.Fori(0, (last - first) // 2) as pair:
                for u in range(2):
                    step(2 * pair + (first + u), (first + u) % 2, lambda off: True)
            for s in range(last, B + 3):
                step(s, s % 2, lambda off, s=s: 0 <= s + off < B)


        block = ctx.enter_context(nc.Block())

        @block.sync
        def _(sp):
            sp.dma_start(adj_i, adj.rearrange("(t p) s -> p t s", p=P)).then_inc(s_adj, 16)
            for b in range(2):
                sp.dma_start(xin[b][:], x[b].rearrange("(t p) d -> p t d", p=P)).then_inc(s_x[b], 16)
            with sp.Fori(1, B // 2) as pair:
                for parity in range(2):
                    b = 2 * pair + parity
                    sp.wait_ge(s_xb, b - 1)
                    hold(sp)
                    sp.wait_ge(s_xn, NT * (b - 1))
                    hold(sp)
                    sp.dma_start(xin[parity][:], x[b].rearrange("(t p) d -> p t d", p=P)).then_inc(s_x[parity], 16)

            def load_expert(e, i):
                sp.dma_start(stage[:, i, 0:W1N].rearrange("p (k n) -> p k n", k=KD),
                             w1[e].rearrange("(k p) n -> p k n", p=P)).then_inc(s_raw[i], 16)
                sp.dma_start(stage[:, i, W1N:].rearrange("p (k n) -> p k n", k=KH),
                             w2[e].rearrange("(k p) n -> p k n", p=P)).then_inc(s_raw[i], 16)

            sp.wait_ge(s_adjt, NT)
            sp.wait_ge(s_big, 2)
            sp.wait_ge(s_adjf, NT)
            for i in range(2):
                load_expert(i, i)
            sp.wait_ge(s_table, TABLE)
            sp.wait_ge(s_const, CONSTS)
            with sp.Fori(0, E) as e:
                end = sp.value_load(table_i[0:1, 3, bass.ds(e, 1)], min_val=0, max_val=E * CAP - TILE)
                sp.dma_start(rows[bass.ds(end, TILE), :].rearrange("(t p) n -> p t n", p=P),
                             filling[:]).then_inc(s_fill, 16)
            sp.wait_ge(s_fill, 16 * E)
            for i in range(2):
                sp.wait_ge(s_sc[i], 16 * NT * B // 2)

            def load_tile(g, row):
                sp.wait_ge(s_free, 2 * g + 2)
                hold(sp)
                sp.wait_ge(s_rt, 16 * (g + 1))
                hold(sp)
                sp.dma_start(rt[:, bass.ds(g % RING, 1), :, :].rearrange("p a t n -> p (a t) n"),
                             rows[bass.ds(row, TILE), :].rearrange("(t p) n -> p t n", p=P)).then_inc(s_rt, 16)

            sp.sem_inc(s_rt, 16)
            with sp.Fori(0, E // 2) as pair:
                for i in range(2):
                    e = 2 * pair + i
                    tiles = sp.value_load(table_i[0:1, 1, bass.ds(e, 1)], min_val=1, max_val=T // TILE)
                    base = sp.value_load(table_i[0:1, 2, bass.ds(e, 1)], min_val=0, max_val=T // TILE + E)
                    with sp.Fori(0, tiles) as n:
                        g = base + n
                        load_tile(g, e * CAP + n * TILE)
                    with sp.If(e < E - 2):
                        sp.wait_ge(s_ewl, e + 1)
                        hold(sp)
                        load_expert((e + 2) % E, i)
            total = sp.value_load(table_i[0:1, 2, E - 1:E], min_val=0, max_val=T // TILE + E) + sp.value_load(
                table_i[0:1, 1, E - 1:E], min_val=1, max_val=T // TILE)
            for n in range(2):
                load_tile(total + n, 0)
            sp.wait_ge(s_rt, 16 * (total + 3))
            hold(sp)
            sp.wait_ge(s_out, 16 * TH * (total + 1))
            hold(sp)

        @block.tensor
        def _(pe):
            pe.wait_ge(s_ident, 1)
            pe.wait_ge(s_adjf, NT)
            for j in range(NT):
                for i in range(NT):
                    m = pe.transpose(agg_ps[j // 2][:, j % 2, i * P:(i + 1) * P], adj_f[:, i, j * P:(j + 1) * P], ident[:])
                m.then_inc(s_adjt, 1)
            pe.wait_ge(s_gw, 16)
            for c in range(2 * KD):
                for o in range(KD):
                    m = pe.transpose(fin_ps[:, c, o * P:(o + 1) * P], gw_n[:, o, c * P:(c + 1) * P], ident[:])
            m.then_inc(s_gwt, 1)
            pe.wait_ge(s_small, 16 * SMALL)
            pe.transpose(b1t_ps, b1_n[:], ident[0:E * KH, 0:E * KH]).then_inc(s_b1t, 1)
            pe.wait_ge(s_big, 7)
            pe.wait_ge(s_ones, 1)
            pe.matmul(big_ps, big[:, 6:7], ones_f[:], start=True, stop=True).then_inc(s_bigp, 1)
            pe.wait_ge(s_bigi, 1)
            large = pe.value_load(big_i[0:1, 0:1], min_val=0, max_val=P)
            pe.wait_ge(s_adjl, NT)
            pe.wait_ge(s_degl, 1)
            pe.wait_ge(s_gwl, 1)
            pe.wait_ge(s_ident_r, 1)
            pe.wait_ge(s_b1, 1)
            pe.wait_ge(s_const, CONSTS)

            def aggregate_by(p, d, parts):
                last = (len(parts) - 1, 1, NT - 1)
                for j in range(NT):
                    for q, xpart in enumerate((xn_h[p], xn_l[p])):
                        xw = xpart[:, j, d * P:(d + 1) * P]
                        for a, (adj_part, deg_part) in enumerate(parts):
                            pe.matmul(agg_ps[d][:, 0, j * P:(j + 1) * P], xw, deg_part[:, j, :],
                                      start=(a == 0 and q == 0), stop=((a, q) == last[:2]))
                            m = pe.matmul(agg_ps[d][:, 1, :], xw, adj_part[:, j, :],
                                          start=((a, q, j) == (0, 0, 0)), stop=((a, q, j) == last))
                m.then_inc(s_agg, 1)

            def aggregate(b, p, d):
                with pe.If(large > 0):
                    aggregate_by(p, d, [(adj_h, deg_h), (adj_l, deg_l)])
                with pe.Else():
                    aggregate_by(p, d, [(adj_h, deg_h)])

            def weight_products(p, t):
                n = 0
                for w in range(2):
                    for d in range(KD):
                        for hl, gws in ((0, (gw_h, gw_l)), (1, (gw_h,))):
                            for gw in gws:
                                m = pe.matmul(fin_ps[:, t, :], ag[p][hl][:, d, w, t * P:(t + 1) * P],
                                              gw[:, w * KD + d, :], start=(n == 0), stop=(n == 6 * KD - 1))
                                n += 1
                m.then_inc(s_fin, 1)

            def transpose_half(h):
                for t in range(HALF):
                    for d in range(KD):
                        o = (t * KD + d) * P
                        for q, part in enumerate((xm_h, xm_l)):
                            m = pe.matmul(tr_ps[:, o:o + P], part[:, h * HALF + t, d * P:(d + 1) * P], ident_r[:],
                                          start=(q == 0), stop=(q == 1))
                m.then_inc(s_tr, 1)

            def step(s, p, has):
                q = 1 - p
                if has(-3):
                    b = s - 3
                    pe.wait_ge(s_gate, 6 * (b + 1))
                    if later(b):
                        pe.wait_ge(s_seen, 2 * b)
                    r = rank_ps.rearrange("p (t e) -> p t e", t=NT)
                    pe.matmul(rank_ps, before_b[:], chosen[q][:].rearrange("p t e -> p (t e)"), start=True, stop=False)
                    pe.matmul(r, ones_b[:], seen[q][:].unsqueeze(1).to_broadcast([P, NT, E]), start=False, stop=False)
                    for t in range(NT - 1):
                        m = pe.matmul(r[:, t + 1:, :], ones_b[:],
                                      chosen[q][:, t:t + 1, :].to_broadcast([P, NT - 1 - t, E]),
                                      start=False, stop=(t == NT - 2))
                    m.then_inc(s_rank, 1)
                if has(0):
                    pe.wait_ge(s_xnl, s + 1)
                    if later(s):
                        pe.wait_ge(s_agl, 2 * s)
                    hold(pe)
                    for d in range(KD):
                        aggregate(s, p, d)
                for t in range(NT):
                    if has(-1):
                        b = s - 1
                        if t == 0:
                            pe.wait_ge(s_agl, 2 * (b + 1))
                        if t % HALF == 0 and later(b):
                            pe.wait_ge(s_x1, 2 * b - 1 + t // HALF)
                        weight_products(q, t)
                    if has(-2) and t < 2:
                        b = s - 2
                        if t == 0:
                            pe.wait_ge(s_xml, b + 1)
                        if t or later(b):
                            pe.wait_ge(s_xmt, 2 * b + t)
                        transpose_half(t)
                    if has(-2) and t == 2:
                        b = s - 2
                        pe.wait_ge(s_xmt, 2 * (b + 1))
                        if later(b):
                            pe.wait_ge(s_slot, 4 * b)
                        for u in range(NT):
                            for d in range(KD):
                                o = (u % HALF * KD + d) * P
                                m = pe.matmul(logit_ps[:, u * E:(u + 1) * E], xm_t[:, u // HALF, o:o + P], wg_sb[:, d, :],
                                              start=(d == 0), stop=(d == KD - 1))
                        m.then_inc(s_log, 1)

            stages(step, pe)

            pe.wait_ge(s_seen, 2 * B)
            pe.wait_ge(s_slot, 4 * B)
            pe.matmul(total_ps, ones_b[:], seen[B % 2][:], start=True, stop=True).then_inc(s_total, 1)

            pe.wait_ge(s_table, TABLE)

            def transpose_rows(g):
                pe.wait_ge(s_znl, g + 1)
                for bank, part in ((th_ps, zn_h), (tl_ps, zn_l)):
                    for t in range(TH):
                        for d in range(KD):
                            o = d * TILE + t * P
                            m = pe.matmul(bank[:, o:o + P], part[:, t, d * P:(d + 1) * P], ident_r[:],
                                          start=True, stop=True)
                m.then_inc(s_zt, 1)

            def ffn(g, i):
                pe.wait_ge(s_zth, g + 1)
                pe.wait_ge(s_ztl, g + 1)
                for c in range(KH):
                    n = 0
                    for d in range(KD):
                        for w, zts in ((w1_h[i], (zt_h, zt_l)), (w1_l[i], (zt_h,))):
                            for zt in zts:
                                m = pe.matmul(h_ps[c], w[:, d, c * P:(c + 1) * P], zt[:, d, :],
                                              start=(n == 0), stop=(n == 3 * KD - 1))
                                n += 1
                    m.then_inc(s_h, 1)
                pe.wait_ge(s_y, TH * (g + 1))
                for c in range(KH):
                    if c == 2:
                        transpose_rows(g + 1)
                    if c < 2:
                        pe.wait_ge(s_hl01, 2 * g + c + 1)
                    else:
                        pe.wait_ge(s_hl23, 2 * g + c - 1)
                    for t in range(TH):
                        for hid, ws in ((hh, (w2_h[i], w2_l[i])), (hl_, (w2_h[i],))):
                            for k, w in enumerate(ws):
                                m = pe.matmul(y_ps[t], hid[:, c, t * P:(t + 1) * P], w[:, c, :],
                                              start=(c == 0 and hid is hh and k == 0), stop=(c == KH - 1 and hid is hl_))
                        if c == KH - 1:
                            m.then_inc(s_yp, 1)

            transpose_rows(0)
            with pe.Fori(0, E // 2) as pair:
                for i in range(2):
                    e = 2 * pair + i
                    tiles = pe.value_load(table_i[0:1, 1, bass.ds(e, 1)], min_val=1, max_val=T // TILE)
                    base = pe.value_load(table_i[0:1, 2, bass.ds(e, 1)], min_val=0, max_val=T // TILE + E)
                    pe.wait_ge(s_ewl, e + 1)
                    hold(pe)
                    with pe.Fori(0, tiles) as n:
                        ffn(base + n, i)

        @block.scalar
        def _(act):
            act.dma_start(gw_n[:], gnn_w.rearrange("(o p) n -> p o n", p=P)).then_inc(s_gw, 16)
            act.dma_start(gb[:], gnn_b.unsqueeze(0).to_broadcast([P, D])).then_inc(s_small, 16)
            act.dma_start(b1_n[:], b1.rearrange("e (k p) -> (e k) p", p=P)).then_inc(s_small, 16)
            with nc.allow_non_contiguous_dma(reason="eight columns"):
                act.dma_start(wg_sb[:], wg.rearrange("(k p) e -> p k e", p=P)).then_inc(s_small, 16)
            act.dma_start(bg_sb[:], bg.unsqueeze(0).to_broadcast([P, E])).then_inc(s_small, 16)
            for i in range(2):
                n = E // 2
                act.dma_start(b2_sb[:, i * n * D:(i + 1) * n * D],
                              b2[i * n:(i + 1) * n].rearrange("e d -> (e d)").unsqueeze(0).to_broadcast([P, n * D])).then_inc(s_small, 16)
            act.wait_ge(s_adj, 16)
            for t in range(NT):
                act.activation(adj_f[:, t, :], adj_i[:, t, :], ACT.Copy, accum_out=deg[:, t:t + 1]).then_inc(s_adjf, 1)
            act.wait_ge(s_ident, 1)
            act.activation(ident_r[:], ident[:], ACT.Copy).then_inc(s_ident_r, 1)
            act.wait_ge(s_degf, NT)
            act.activation(deg_h[:], deg_f[:], ACT.Copy).then_inc(s_degh, 1)
            for j in range(NT):
                act.wait_ge(s_adjt, j + 1)
                act.activation(adj_h[:, j, :], agg_ps[j // 2][:, j % 2, :], ACT.Copy).then_inc(s_adjh, 1)
            act.wait_ge(s_gwt, 1)
            act.activation(gw_h[:], fin_ps[:], ACT.Copy).then_inc(s_gwh, 1)
            act.wait_ge(s_b1t, 1)
            act.activation(b1_t[:], b1t_ps, ACT.Copy).then_inc(s_b1, 1)

            def step(s, p, has):
                q = 1 - p
                if has(-2):
                    b = s - 2
                    act.wait_ge(s_sh2, b + 1)
                    if later(b):
                        act.wait_ge(s_xml, b)
                        act.wait_ge(s_xmh, b)
                    for t in range(NT):
                        act.activation(xm[:, t, :], x1[p][:, t, 0:D], ACT.Identity, scale=rs2[:, t:t + 1],
                                       bias=sh2[:, t:t + 1]).then_inc(s_xm, 1)
                    act.wait_ge(s_xm, NT * (b + 1))
                    if later(b):
                        act.wait_ge(s_tr, 2 * b)
                    act.activation(xm_h[:], xm[:], ACT.Copy).then_inc(s_xmh, 1)
                if has(0):
                    act.wait_ge(s_agg, 2 * s + 1)
                    if reused(s):
                        act.wait_ge(s_fin, NT * (s - 1))
                    act.activation(ag[p][0][:, 0], agg_ps[0][:], ACT.Copy).then_inc(s_agh, 1)
                if has(1):
                    b = s + 1
                    act.wait_ge(s_sh1, b + 1)
                    if later(b):
                        act.wait_ge(s_xnl, b)
                        act.wait_ge(s_xnh, b)
                    for t in range(NT):
                        act.activation(xn[:, t, :], xin[q][:, t, :], ACT.Identity, scale=rs1[:, t:t + 1],
                                       bias=sh1[:, t:t + 1]).then_inc(s_xn, 1)
                    act.wait_ge(s_xn, NT * (b + 1))
                    if reused(b):
                        act.wait_ge(s_agg, 2 * (b - 1))
                    act.activation(xn_h[q][:], xn[:], ACT.Copy).then_inc(s_xnh, 1)
                if has(-2):
                    b = s - 2
                    for h in range(2):
                        act.wait_ge(s_tr, 2 * b + h + 1)
                        if later(b):
                            act.wait_ge(s_log, b)
                        act.activation(xm_t[:, h, :], tr_ps[:], ACT.Copy).then_inc(s_xmt, 1)
                if has(0):
                    act.wait_ge(s_agg, 2 * s + 2)
                    act.activation(ag[p][0][:, 1], agg_ps[1][:], ACT.Copy).then_inc(s_agh, 1)

            stages(step, act)

            act.wait_ge(s_table, TABLE)

            def split_weights(e, i, base):
                act.wait_ge(s_raw[i], nth_of_parity(e, i, 32))
                if base is None:
                    act.wait_ge(s_fin, NT * B)
                else:
                    act.wait_ge(s_y, TH * (base + 1))
                act.activation(ew_h[i], stage[:, i, :], ACT.Copy).then_inc(s_ewh, 1)

            def normalise(g):
                act.wait_ge(s_sh3, g + 1)
                if later(g):
                    act.wait_ge(s_znl, g)
                    act.wait_ge(s_znh, g)
                for t in range(TH):
                    act.activation(zn[:, t, :], rt[:, bass.ds(g % RING, 1), t, 0:D].rearrange("p a d -> p (a d)"), ACT.Identity, scale=rs3[:, t:t + 1],
                                   bias=sh3[:, t:t + 1]).then_inc(s_zn, 1)
                act.wait_ge(s_zn, TH * (g + 1))
                if later(g):
                    act.wait_ge(s_zt, g)
                act.activation(zn_h[:], zn[:], ACT.Copy).then_inc(s_znh, 1)

            def copy_transposed(g):
                act.wait_ge(s_zt, g + 1)
                act.activation(zt_h[:].rearrange("p k n -> p (k n)"), th_ps[:], ACT.Copy).then_inc(s_zth, 1)

            split_weights(0, 0, None)
            normalise(0)
            copy_transposed(0)
            with act.Fori(0, E // 2) as pair:
                for i in range(2):
                    e = 2 * pair + i
                    tiles = act.value_load(table_i[0:1, 1, bass.ds(e, 1)], min_val=1, max_val=T // TILE)
                    base = act.value_load(table_i[0:1, 2, bass.ds(e, 1)], min_val=0, max_val=T // TILE + E)
                    with act.If(e < E - 1):
                        split_weights(e + 1, 1 - i, base)
                    with act.Fori(0, tiles) as n:
                        g = base + n
                        normalise(g + 1)
                        for c in range(KH):
                            act.wait_ge(s_h, KH * g + c + 1)
                            act.activation(hr[:, c, :], h_ps[c], ACT.Relu,
                                           bias=b1_t[:, bass.ds(e * KH + c, 1)]).then_inc(s_hr, 1)
                        copy_transposed(g + 1)

        @block.vector
        def _(dve):
            dve.wait_ge(s_adj, 16)
            for i, op in enumerate((ALU.max, ALU.min)):
                dve.tensor_reduce(big[:, 2 * i:2 * i + 1], adj_i.rearrange("p t s -> p (t s)"), AX_X, op).then_inc(s_big, 1)
            dve.wait_ge(s_adjf, NT)
            dve.wait_ge(s_ident, 1)
            for t in range(NT):
                dve.tensor_scalar(deg_f[:, t, :], ident[:], deg[:, t:t + 1], None, ALU.mult).then_inc(s_degf, 1)
            for i, op in enumerate((ALU.max, ALU.min)):
                dve.tensor_reduce(big[:, 2 * i + 1:2 * i + 2], deg[:], AX_X, op).then_inc(s_big, 1)
            dve.wait_ge(s_big, 4)
            dve.tensor_scalar(big[:, 4:5], big[:, 0:1], big[:, 1:2], None, ALU.max).then_inc(s_big, 1)
            dve.tensor_scalar(big[:, 5:6], big[:, 2:3], big[:, 3:4], -1.0, ALU.min, ALU.mult).then_inc(s_big, 1)
            dve.wait_ge(s_big, 6)
            dve.tensor_scalar(big[:, 6:7], big[:, 4:5], big[:, 5:6], EXACT, ALU.max, ALU.is_gt).then_inc(s_big, 1)
            dve.wait_ge(s_bigp, 1)
            dve.tensor_copy(big_i[:], big_ps).then_inc(s_bigi, 1)
            dve.wait_ge(s_degh, 1)
            dve.wait_ge(s_degf, NT)
            dve.tensor_tensor(deg_l[:], deg_f[:], deg_h[:].bitcast(F32), ALU.subtract).then_inc(s_degl, 1)

            def statistics1(b, p):
                dve.wait_ge(s_x[p], nth_of_parity(b, p, 16))
                if later(b):
                    dve.wait_ge(s_ve1, 2 * b)
                    dve.wait_ge(s_mv1, NT * b)
                for t in range(NT):
                    dve.bn_stats(st1[:, t, :], xin[p][:, t, :]).then_inc(s_bn1, 1)
                dve.wait_ge(s_bn1, NT * (b + 1))
                hold(dve)
                for t in range(NT):
                    dve.bn_aggr(mv1[:, t, :], st1[:, t, :]).then_inc(s_mv1, 1)
                dve.wait_ge(s_mv1, NT * (b + 1))
                if later(b):
                    dve.wait_ge(s_sh1, b)
                dve.tensor_scalar(ve1[:], mv1[:, :, 1], EPS, None, ALU.add).then_inc(s_ve1, 1)
                dve.tensor_scalar(nm1[:], mv1[:, :, 0], -1.0, None, ALU.mult).then_inc(s_ve1, 1)

            def low_aggregate(s, p, d):
                dve.wait_ge(s_agh, 2 * s + d + 1)
                dve.tensor_tensor(ag[p][1][:, d], agg_ps[d][:], ag[p][0][:, d].bitcast(F32),
                                  ALU.subtract).then_inc(s_agl, 1)

            def step(s, p, has):
                q = 1 - p
                if has(-3):
                    b = s - 3
                    dve.wait_ge(s_rank, b + 1)
                    if later(b):
                        dve.wait_ge(s_slot, 4 * b)
                    dve.tensor_tensor(flat(place[:]), rank_ps, flat(region[:]), ALU.add).then_inc(s_slot, 1)
                    dve.wait_ge(s_slot, 4 * b + 1)
                    dve.tensor_tensor(place[:], place[:], chosen[q][:], ALU.mult).then_inc(s_slot, 1)
                    dve.wait_ge(s_slot, 4 * b + 2)
                    dve.tensor_reduce(slot[:], place[:], AX_X, ALU.add).then_inc(s_slot, 1)
                    dve.wait_ge(s_slot, 4 * b + 3)
                    if reused(b):
                        dve.wait_ge(s_sc[q], nth_of_parity(b - 2, q, 16 * NT))
                    dve.tensor_copy(slot_i[q][:], slot[:]).then_inc(s_slot, 1)
                if has(1):
                    statistics1(s + 1, q)
                if has(-2):
                    b = s - 2
                    dve.wait_ge(s_xmh, b + 1)
                    if later(b):
                        dve.wait_ge(s_tr, 2 * b)
                    dve.tensor_tensor(xm_l[:], xm[:], xm_h[:].bitcast(F32), ALU.subtract).then_inc(s_xml, 1)
                if has(0):
                    if reused(s):
                        dve.wait_ge(s_fin, NT * (s - 1))
                    low_aggregate(s, p, 0)
                for h in range(2):
                    if has(-1):
                        b = s - 1
                        if h == 0:
                            dve.wait_ge(s_xb, b + 1)
                            if reused(b):
                                dve.wait_ge(s_sc[q], nth_of_parity(b - 2, q, 16 * NT))
                                dve.wait_ge(s_xm, NT * (b - 1))
                        dve.wait_ge(s_fin, NT * b + HALF * (h + 1))
                        ts = slice(h * HALF, (h + 1) * HALF)
                        dve.tensor_tensor(x1[q][:, ts, 0:D], fin_ps[:, ts, :], xb[q][:, ts, :], ALU.add).then_inc(s_x1, 1)
                        dve.wait_ge(s_x1, 2 * b + h + 1)
                        if h == 0 and later(b):
                            dve.wait_ge(s_mv2, NT * b)
                        for t in range(h * HALF, (h + 1) * HALF):
                            dve.bn_stats(st2[:, t, :], x1[q][:, t, 0:D]).then_inc(s_bn2, 1)
                        if h == 1:
                            dve.tensor_copy(x1[q][:, :, D:D + 1].bitcast(I32),
                                            token_no[:, bass.ds(b * NT, NT)].unsqueeze(2)).then_inc(s_no, 1)
                            dve.wait_ge(s_bn2, NT * (b + 1))
                            if later(b):
                                dve.wait_ge(s_ve2, 2 * b)
                            hold(dve)
                            for t in range(NT):
                                dve.bn_aggr(mv2[:, t, :], st2[:, t, :]).then_inc(s_mv2, 1)
                            dve.wait_ge(s_mv2, NT * (b + 1))
                            if later(b):
                                dve.wait_ge(s_sh2, b)
                            dve.tensor_scalar(ve2[:], mv2[:, :, 1], EPS, None, ALU.add).then_inc(s_ve2, 1)
                            dve.tensor_scalar(nm2[:], mv2[:, :, 0], -1.0, None, ALU.mult).then_inc(s_ve2, 1)
                    if h == 0 and has(-2):
                        b = s - 2
                        g = 6 * b
                        dve.wait_ge(s_log, b + 1)
                        if later(b):
                            dve.wait_ge(s_gate, g)
                        dve.tensor_tensor(logit[:], logit_ps.rearrange("p (t e) -> p t e", t=NT),
                                          bg_sb[:].unsqueeze(1).to_broadcast([P, NT, E]), ALU.add).then_inc(s_gate, 1)
                        dve.wait_ge(s_gate, g + 1)
                        dve.tensor_reduce(top[:], logit[:], AX_X, ALU.max).then_inc(s_gate, 1)
                        dve.wait_ge(s_gate, g + 2)
                        dve.tensor_tensor(score[:], logit[:], top[:].unsqueeze(2).to_broadcast([P, NT, E]),
                                          ALU.is_equal).then_inc(s_gate, 1)
                        dve.wait_ge(s_gate, g + 3)
                        dve.tensor_tensor(score[:], score[:], order[:], ALU.mult).then_inc(s_gate, 1)
                        dve.wait_ge(s_gate, g + 4)
                        dve.tensor_reduce(best[:], score[:], AX_X, ALU.max).then_inc(s_gate, 1)
                        dve.wait_ge(s_gate, g + 5)
                        if reused(b):
                            dve.wait_ge(s_slot, 4 * (b - 1))
                            dve.wait_ge(s_rank, b - 1)
                            dve.wait_ge(s_seen, 2 * (b - 1))
                        dve.tensor_tensor(chosen[p][:], score[:], best[:].unsqueeze(2).to_broadcast([P, NT, E]),
                                          ALU.is_equal).then_inc(s_gate, 1)
                        dve.wait_ge(s_gate, g + 6)
                        if later(b):
                            dve.wait_ge(s_seen, 2 * b)
                        dve.tensor_reduce(added[:], chosen[p][:].rearrange("p t e -> p e t"), AX_X,
                                          ALU.add).then_inc(s_seen, 1)
                        dve.wait_ge(s_seen, 2 * b + 1)
                        if later(b):
                            dve.wait_ge(s_rank, b)
                        dve.tensor_tensor(seen[q][:], seen[p][:], added[:], ALU.add).then_inc(s_seen, 1)
                if has(0):
                    low_aggregate(s, p, 1)

            statistics1(0, 0)
            for j in range(NT):
                dve.wait_ge(s_adjh, j + 1)
                dve.tensor_tensor(adj_l[:, j, :], agg_ps[j // 2][:, j % 2, :], adj_h[:, j, :].bitcast(F32),
                                  ALU.subtract).then_inc(s_adjl, 1)
            dve.wait_ge(s_gwh, 1)
            dve.tensor_tensor(gw_l[:], fin_ps[:], gw_h[:].bitcast(F32), ALU.subtract).then_inc(s_gwl, 1)
            dve.wait_ge(s_const, CONSTS)
            stages(step, dve, 0)

            dve.wait_ge(s_total, 1)
            dve.tensor_copy(table_i[:, 0, :], total_ps).then_inc(s_table, 1)
            dve.tensor_tensor(table_i[:, 3, :], total_ps, region[:, 0, :], ALU.add).then_inc(s_table, 1)
            dve.wait_ge(s_table, 2)
            dve.tensor_scalar(table_i[:, 2, :], table_i[:, 0, :], 1.0, 0.0, ALU.subtract, ALU.max).then_inc(s_table, 1)
            dve.wait_ge(s_table, 3)
            shift = TILE.bit_length() - 1
            dve.tensor_scalar(table_i[:, 1, :], table_i[:, 2, :], shift, None, ALU.logical_shift_right).then_inc(s_table, 1)
            dve.wait_ge(s_table, 4)
            dve.tensor_scalar(table_i[:, 1, :], table_i[:, 1, :], 1.0, None, ALU.add).then_inc(s_table, 1)
            dve.wait_ge(s_table, 5)
            dve.tensor_copy(table_f[:, 0, :], table_i[:, 1, :]).then_inc(s_base, 1)
            dve.memset(table_f[:, 1, 0:1], 0.0).then_inc(s_base, 1)
            for e in range(1, E):
                dve.wait_ge(s_base, 1 + e)
                dve.tensor_tensor(table_f[:, 1, e:e + 1], table_f[:, 1, e - 1:e], table_f[:, 0, e - 1:e],
                                  ALU.add).then_inc(s_base, 1)
            dve.wait_ge(s_base, 1 + E)
            dve.wait_ge(s_table, 5)
            dve.tensor_copy(table_i[:, 2, :], table_f[:, 1, :]).then_inc(s_table, 1)
            dve.wait_ge(s_table, TABLE)

            def split_weights(e, i):
                dve.wait_ge(s_ewh, e + 1)
                dve.tensor_tensor(ew_l[i], stage[:, i, :], ew_h[i].bitcast(F32), ALU.subtract).then_inc(s_ewl, 1)

            def statistics3(g):
                dve.wait_ge(s_rt, 16 * (g + 2))
                if later(g):
                    dve.wait_ge(s_mv3, TH * g)
                for t in range(TH):
                    dve.bn_stats(st3[:, t, :], rt[:, bass.ds(g % RING, 1), t, 0:D].rearrange("p a d -> p (a d)")).then_inc(s_bn3, 1)
                dve.wait_ge(s_bn3, TH * (g + 1))
                if later(g):
                    dve.wait_ge(s_ve3, 2 * g)
                hold(dve)
                for t in range(TH):
                    dve.bn_aggr(mv3[:, t, :], st3[:, t, :]).then_inc(s_mv3, 1)
                dve.wait_ge(s_mv3, TH * (g + 1))
                if later(g):
                    dve.wait_ge(s_sh3, g)
                dve.tensor_scalar(ve3[:], mv3[:, :, 1], EPS, None, ALU.add).then_inc(s_ve3, 1)
                dve.tensor_scalar(nm3[:], mv3[:, :, 0], -1.0, None, ALU.mult).then_inc(s_ve3, 1)

            def low_rows(g):
                dve.wait_ge(s_znh, g + 1)
                if later(g):
                    dve.wait_ge(s_zt, g)
                dve.tensor_tensor(zn_l[:], zn[:], zn_h[:].bitcast(F32), ALU.subtract).then_inc(s_znl, 1)

            def copy_transposed(g):
                dve.wait_ge(s_zt, g + 1)
                dve.tensor_copy(zt_l[:].rearrange("p k n -> p (k n)"), tl_ps[:]).then_inc(s_ztl, 1)

            dve.sem_inc(s_y, TH)
            statistics3(0)
            split_weights(0, 0)
            low_rows(0)
            statistics3(1)
            copy_transposed(0)
            with dve.Fori(0, E // 2) as pair:
                for i in range(2):
                    e = 2 * pair + i
                    tiles = dve.value_load(table_i[0:1, 1, bass.ds(e, 1)], min_val=1, max_val=T // TILE)
                    base = dve.value_load(table_i[0:1, 2, bass.ds(e, 1)], min_val=0, max_val=T // TILE + E)
                    with dve.If(e < E - 1):
                        split_weights(e + 1, 1 - i)
                    with dve.Fori(0, tiles) as n:
                        g = base + n
                        low_rows(g + 1)
                        for c in range(KH):
                            dve.wait_ge(s_hr, KH * g + c + 1)
                            dve.tensor_copy(hh[:, c, :], hr[:, c, :]).then_inc(s_hh, 1)
                            if c < 2:
                                dve.wait_ge(s_hh, KH * g + c + 1)
                                dve.tensor_tensor(hl_[:, c, :], hr[:, c, :], hh[:, c, :].bitcast(F32),
                                                  ALU.subtract).then_inc(s_hl01, 1)
                        statistics3(g + 2)
                        copy_transposed(g + 1)
                        dve.wait_ge(s_out, 16 * TH * (g + 1))
                        dve.wait_ge(s_free, 2 * (g + 1 + RING))
                        dve.tensor_copy(tok[:], tok_early[:]).then_inc(s_tok, 1)
                        for t in range(TH):
                            dve.wait_ge(s_yp, TH * g + t + 1)
                            dve.tensor_tensor(y[:, t, :], y_ps[t], res[:, t, :], ALU.add).then_inc(s_y, 1)

        @block.gpsimd
        def _(pool):
            pool.memset(ident[:], 0.0).then_inc(s_zero, 1)
            pool.wait_ge(s_zero, 1)
            pool.affine_select(out=ident[:], in_=ident[:], compare_op=ALU.not_equal, fill=1.0, base=0,
                               pattern=[[-1, P]], channel_multiplier=1).then_inc(s_ident, 1)
            pool.memset(ones_f[:], 1.0).then_inc(s_ones, 1)
            pool.memset(minus_half[:], -0.5).then_inc(s_half, 1)

            def shift(ve, nm, rs, sh, s_rs, s_sh, b, n):
                pool.tensor_tensor(rs[:], ve[:], minus_half[:, 0:n], ALU.pow).then_inc(s_rs, 1)
                pool.wait_ge(s_rs, b + 1)
                pool.tensor_tensor(sh[:], nm[:], rs[:], ALU.mult).then_inc(s_sh, 1)

            def shift1(b):
                pool.wait_ge(s_ve1, 2 * (b + 1))
                if later(b):
                    pool.wait_ge(s_xn, NT * b)
                shift(ve1, nm1, rs1, sh1, s_rs1, s_sh1, b, NT)

            pool.wait_ge(s_half, 1)
            shift1(0)
            pool.memset(ones_b[:], 1.0).then_inc(s_zero, 1)
            pool.memset(before_b[:], 1.0).then_inc(s_zero, 1)
            pool.memset(filling[:], 0.0).then_inc(s_zero, 1)
            pool.iota(region_i[:], [[0, NT], [CAP, E]], base=0, channel_multiplier=0).then_inc(s_zero, 1)
            pool.iota(order_i[:], [[0, NT], [-1, E]], base=E, channel_multiplier=0).then_inc(s_zero, 1)
            pool.wait_ge(s_zero, 6)
            pool.affine_select(out=before_b[:], in_=before_b[:], compare_op=ALU.is_gt, fill=0.0, base=0,
                               pattern=[[1, P]], channel_multiplier=-1).then_inc(s_const, 1)
            pool.memset(filling[:, :, D:D + 1].bitcast(I32), NO_TOKEN).then_inc(s_const, 1)
            pool.tensor_copy(region[:], region_i[:]).then_inc(s_const, 1)
            pool.tensor_copy(order[:], order_i[:]).then_inc(s_const, 1)
            pool.iota(token_no[:], [[P, T // P]], base=0, channel_multiplier=1).then_inc(s_const, 1)
            pool.memset(seen[0][:], 0.0).then_inc(s_const, 1)
            for i in range(2):
                pool.memset(x1[i][:, :, D:], 0.0).then_inc(s_const, 1)
            pool.wait_ge(s_small, 16 * SMALL)
            pool.wait_ge(s_adjf, NT)
            for t in range(NT):
                pool.tensor_scalar(deg_b[:, t, :], gb[:], deg[:, t:t + 1], None, ALU.mult).then_inc(s_degb, 1)
            pool.wait_ge(s_degb, NT)
            pool.wait_ge(s_const, CONSTS)

            def scatter_rows(b, i, t):
                pool.indirect_dma_start(out=rows, out_offset=bass.IndirectOffsetOnAxis(ap=slot_i[i][:, t:t + 1].bitcast(U32), axis=0),
                                        in_=x1[i][:, t, :], in_offset=None, bounds_check=E * CAP - 1,
                                        oob_is_err=False).then_inc(s_sc[i], 16)

            def step(s, p, has):
                q = 1 - p
                if has(-2):
                    b = s - 2
                    pool.wait_ge(s_ve2, 2 * (b + 1))
                    if later(b):
                        pool.wait_ge(s_xm, NT * b)
                    shift(ve2, nm2, rs2, sh2, s_rs2, s_sh2, b, NT)
                if has(-3):
                    pool.wait_ge(s_slot, 4 * (s - 3 + 1))
                    pool.wait_ge(s_no, s - 3 + 1)
                    hold(pool)
                    scatter_rows(s - 3, q, 0)
                if has(1) and has(0):
                    shift1(s + 1)
                if has(-3):
                    for t in range(1, NT):
                        scatter_rows(s - 3, q, t)
                if has(0):
                    pool.wait_ge(s_x[p], nth_of_parity(s, p, 16))
                    if reused(s):
                        pool.wait_ge(s_x1, 2 * (s - 1))
                    pool.tensor_tensor(xb[p][:], xin[p][:], deg_b[:], ALU.add).then_inc(s_xb, 1)
                if has(1):
                    b = s + 1
                    pool.wait_ge(s_xnh, b + 1)
                    if reused(b):
                        pool.wait_ge(s_agg, 2 * (b - 1))
                    pool.tensor_tensor(xn_l[q][:], xn[:], xn_h[q][:].bitcast(F32), ALU.subtract).then_inc(s_xnl, 1)

            stages(step, pool)

            pool.wait_ge(s_table, TABLE)
            pool.sem_inc(s_free, 2 * RING)
            pool.sem_inc(s_tok, 1)

            def scatter_out(values, tokens):
                pool.indirect_dma_start(out=out_rows, out_offset=bass.IndirectOffsetOnAxis(ap=tokens.bitcast(U32), axis=0),
                                        in_=values, in_offset=None, bounds_check=T - 1,
                                        oob_is_err=False).then_inc(s_out, 16)

            for t in range(TH):
                scatter_out(filling[:, t, 0:D], filling[:, t, D:D + 1])

            def shift3(g):
                pool.wait_ge(s_ve3, 2 * (g + 1))
                if later(g):
                    pool.wait_ge(s_zn, TH * g)
                shift(ve3, nm3, rs3, sh3, s_rs3, s_sh3, g, TH)

            shift3(0)
            shift3(1)
            with pool.Fori(0, E) as e:
                tiles = pool.value_load(table_i[0:1, 1, bass.ds(e, 1)], min_val=1, max_val=T // TILE)
                base = pool.value_load(table_i[0:1, 2, bass.ds(e, 1)], min_val=0, max_val=T // TILE + E)
                with pool.Fori(0, tiles) as n:
                    g = base + n
                    for c in range(2, KH):
                        pool.wait_ge(s_hh, KH * g + c + 1)
                        pool.tensor_tensor(hl_[:, c, :], hr[:, c, :], hh[:, c, :].bitcast(F32), ALU.subtract).then_inc(s_hl23, 1)
                    pool.wait_ge(s_rt, 16 * (g + 2))
                    pool.wait_ge(s_y, TH * (g + 1))
                    hold(pool)
                    pool.tensor_tensor(res[:], rt[:, bass.ds(g % RING, 1), :, 0:D].rearrange("p a t d -> p (a t) d"),
                                       b2_sb[:, bass.ds(e * D, D)].unsqueeze(1).to_broadcast([P, TH, D]),
                                       ALU.add).then_inc(s_free, 1)
                    pool.wait_ge(s_tok, g + 1)
                    hold(pool)
                    pool.tensor_copy(tok_early[:].unsqueeze(2), rt[:, bass.ds(g % RING, 1), :, D:D + 1].rearrange("p a t d -> p (a t) d").bitcast(I32)).then_inc(s_free, 1)
                    shift3(g + 2)
                    pool.wait_ge(s_tok, g + 2)
                    for t in range(TH):
                        pool.wait_ge(s_y, TH * (g + 1) + t + 1)
                        hold(pool)
                        scatter_out(y[:, t, :], tok[:, t:t + 1])


def kernel(**inputs):
    import numpy as np
    import concourse.bacc as bacc
    from concourse.bass_utils import run_bass_kernel_spmd

    names = ["x", "adj", "L0_gnn_W", "L0_gnn_b", "L0_ffn_W1", "L0_ffn_b1", "L0_ffn_W2", "L0_ffn_b2", "L0_ffn_Wg", "L0_ffn_bg"]
    nc = bacc.Bacc("TRN2", target_bir_lowering=False, num_devices=1)
    arrays, args = {}, []
    for name in names:
        a = np.ascontiguousarray(inputs[name])
        arrays[name] = a
        args.append(nc.dram_tensor(name, a.shape, mybir.dt.from_np(a.dtype), kind="ExternalInput").ap())
    args.append(nc.dram_tensor("out", arrays["x"].shape, F32, kind="ExternalOutput").ap())
    moe_gnn_kernel(nc, *args)
    return run_bass_kernel_spmd(nc, [arrays], core_ids=[0]).results[0]["out"]
```

```python
from contextlib import ExitStack

import concourse.bass as bass
from concourse import mybir

F32 = mybir.dt.float32
F32R = mybir.dt.float32r
BF16 = mybir.dt.bfloat16
I32 = mybir.dt.int32
U32 = mybir.dt.uint32
ALU = mybir.AluOpType
ACT = mybir.ActivationFunctionType
AX_X = mybir.AxisListType.X

P = 128
EPS = 1e-5
PAD = 4
TILE = 256
RING = 8
QUARTERS = 4
NO_TOKEN = 1 << 20
EXACT = 4096.0


def moe_gnn_kernel(nc, x, adj, gnn_w, gnn_b, w1, b1, w2, b2, wg, bg, out):
    B, S, D = x.shape
    E, _, H = w1.shape
    T = B * S
    NT = S // P
    KD = D // P
    KH = H // P
    TH = TILE // P
    CAP = T + TILE
    ROW = D + PAD
    HALF = NT // 2
    HALF_H = KH // 2
    W1N, W2N = KD * H, KH * D
    QN = (W1N + W2N) // QUARTERS
    assert S == 512 and KD == 2 and KH == 4 and NT == 4 and B % 2 == 0 and B >= 8

    rows = nc.dram_tensor("expert_rows", (E * CAP, ROW), F32, kind="Internal").ap()
    out_rows = out.rearrange("b s d -> (b s) d")

    with ExitStack() as ctx:
        def sb(name, shape, dt=F32):
            return ctx.enter_context(nc.sbuf_tensor(name, shape, dt))

        def ps(name, shape):
            return ctx.enter_context(nc.psum_tensor(name, shape, F32))

        def sem(name):
            return ctx.enter_context(nc.semaphore(name))

        agg_ps = [ps(f"agg_ps{d}", [P, 2, S]) for d in range(KD)]
        fin_ps = ps("fin_ps", [P, NT, D])
        tr_ps = ps("tr_ps", [P, S])
        misc_ps = ps("misc_ps", [P, S])
        h_ps = [agg_ps[0][:, 0, 0:TILE], agg_ps[0][:, 1, 0:TILE], agg_ps[1][:, 0, 0:TILE], agg_ps[1][:, 1, 0:TILE]]
        y_ps = [fin_ps[:, 0, :], fin_ps[:, 2, :]]
        th_ps, tl_ps = tr_ps, misc_ps
        logit_ps = misc_ps[:, 0:NT * E]
        rank_ps = misc_ps[:, 64:64 + NT * E]
        total_ps = misc_ps[:, 128:128 + E]
        adjt_ps = [fin_ps[:, 0:HALF, :].rearrange("p t d -> p (t d)"), fin_ps[:, HALF:, :].rearrange("p t d -> p (t d)"),
                   tr_ps[:], misc_ps[:]]
        gwt_ps = agg_ps[1][:].rearrange("p w (c d) -> p (w c) d", d=D)
        b1t_ps = agg_ps[0][:, 0, 0:E * KH]
        big_ps = agg_ps[0][0:1, 1, 0:1]

        ident = sb("ident", [P, P])
        ident_r = sb("ident_r", [P, P], F32R)
        ones_b = sb("ones_b", [P, P], BF16)
        before_b = sb("before_b", [P, P], BF16)
        ones_f = sb("ones_f", [P, 1])
        minus_half = sb("minus_half", [P, NT])
        token_no = sb("token_no", [P, T // P], I32)
        region = sb("region", [P, NT, E])
        region_i = sb("region_i", [P, NT, E], I32)
        order = sb("order", [P, NT, E])
        order_i = sb("order_i", [P, NT, E], I32)
        filling = sb("filling", [P, TH, ROW])
        SC = S - P
        tile0 = [sb(f"tile0_{n}", [P, 2, S], F32R) for n in ("high", "low")]
        tiles13 = [sb(f"tiles13_{n}", [P, NT - 1, S + P], F32R) for n in ("high", "low")]
        deg = sb("deg", [P, NT])
        deg_f = sb("deg_f", [P, NT, P])
        deg_b = sb("deg_b", [P, NT, D])
        gw_h = sb("gw_h", [P, 2 * KD, D], F32R)
        gw_l = sb("gw_l", [P, 2 * KD, D], F32R)
        gb = sb("gb", [P, D])
        wg_sb = sb("wg_sb", [P, KD, E])
        bg_sb = sb("bg_sb", [P, E])
        b1_n = sb("b1_n", [E * KH, P])
        b1_t = sb("b1_t", [P, E * KH])
        b2_sb = sb("b2_sb", [P, E * D])
        big = sb("big", [P, 4])
        big_i = sb("big_i", [1, 1], I32)
        table_f = sb("table_f", [P, 2, E])
        earlier = sb("earlier", [P, E, E])
        tiles_earlier = sb("tiles_earlier", [P, E, E])
        table_i = sb("table_i", [P, 3, E], I32)
        FIELD = 64
        assert T // TILE + E < FIELD
        pair_f = sb("pair_f", [P, E // 2])
        pair_words = sb("pair_words", [P, E // 2], I32)
        stage = sb("stage", [P, 2, W1N + W2N])
        adj_i = stage[:, 0, :].bitcast(I32).rearrange("p (t s) -> p t s", t=NT)
        adj_f = stage[:, 1, :].rearrange("p (t s) -> p t s", t=NT)
        gw_n = sb("gw_n", [P, KD, 2 * D])

        xin = [sb(f"xin{i}", [P, NT, D]) for i in range(2)]
        xb = [sb(f"xb{i}", [P, NT, D]) for i in range(2)]
        xn = sb("xn", [P, NT, D])
        xn_h = [sb(f"xn_h{i}", [P, NT, D], F32R) for i in range(2)]
        xn_l = [sb(f"xn_l{i}", [P, NT, D], F32R) for i in range(2)]
        split = sb("split", [P, 2, 2, 2 * KD * S], F32R)
        ag = [[split[:, i, hl, :].rearrange("p (d w s) -> p d w s", d=KD, w=2) for hl in range(2)] for i in range(2)]
        rt = sb("rt", [P, RING, TH, ROW])
        x1 = [sb(f"x1_{i}", [P, NT, ROW]) for i in range(2)]
        x1.append(rt[:, RING - NT // TH:].rearrange("p r t n -> p (r t) n"))
        xm = sb("xm", [P, NT, D])
        xm_h = sb("xm_h", [P, NT, D], F32R)
        xm_l = sb("xm_l", [P, NT, D], F32R)
        xm_t = sb("xm_t", [P, 2, S])
        st1 = sb("st1", [P, NT, 6])
        mv1 = sb("mv1", [P, NT, 2])
        ve1 = sb("ve1", [P, NT])
        nm1 = sb("nm1", [P, NT])
        rs1 = sb("rs1", [P, NT])
        sh1 = sb("sh1", [P, NT])
        st2 = sb("st2", [P, NT, 6])
        mv2 = sb("mv2", [P, NT, 2])
        ve2 = sb("ve2", [P, NT])
        nm2 = sb("nm2", [P, NT])
        rs2 = sb("rs2", [P, NT])
        sh2 = sb("sh2", [P, NT])
        logit = sb("logit", [P, NT, E])
        top = sb("top", [P, NT])
        score = sb("score", [P, NT, E])
        best = sb("best", [P, NT])
        chosen = [sb(f"chosen{i}", [P, NT, E], BF16) for i in range(2)]
        seen = [sb(f"seen{i}", [P, E], BF16) for i in range(2)]
        added = sb("added", [P, E])
        place = sb("place", [P, NT, E])
        slot = sb("slot", [P, NT])
        slot_i = [sb(f"slot_i{i}", [P, NT], I32) for i in range(2)]

        zn = sb("zn", [P, TH, D])
        zn_h = sb("zn_h", [P, TH, D], F32R)
        zn_l = sb("zn_l", [P, TH, D], F32R)
        zt_h = sb("zt_h", [P, KD, TILE], F32R)
        zt_l = sb("zt_l", [P, KD, TILE], F32R)
        hr = sb("hr", [P, KH, TILE])
        hh = sb("hh", [P, KH, TILE], F32R)
        hl_ = sb("hl_", [P, KH, TILE], F32R)
        res = sb("res", [P, TH, D])
        y = sb("y", [P, TH, D])
        tok_early = sb("tok_early", [P, TH], I32)
        tok = sb("tok", [P, TH], I32)
        st3 = sb("st3", [P, TH, 6])
        mv3 = sb("mv3", [P, TH, 2])
        ve3 = sb("ve3", [P, TH])
        nm3 = sb("nm3", [P, TH])
        rs3 = sb("rs3", [P, TH])
        sh3 = sb("sh3", [P, TH])
        ew_h = [split[:, i, 0, :] for i in range(2)]
        ew_l = [split[:, i, 1, :] for i in range(2)]
        w1_h = [w[:, 0:W1N].rearrange("p (k n) -> p k n", k=KD) for w in ew_h]
        w1_l = [w[:, 0:W1N].rearrange("p (k n) -> p k n", k=KD) for w in ew_l]
        w2_h = [w[:, W1N:].rearrange("p (k n) -> p k n", k=KH) for w in ew_h]
        w2_l = [w[:, W1N:].rearrange("p (k n) -> p k n", k=KH) for w in ew_l]

        s_adj = [sem(f"adj_loaded{i}") for i in range(2)]
        s_gw = sem("gnn_weights_loaded")
        s_small = sem("small_inputs_loaded")
        s_zero = sem("tiles_set")
        s_zeros = sem("zeros_behind_tile_0")
        s_ident = sem("identity_written")
        s_ones = sem("ones_written")
        s_half = sem("minus_half_written")
        s_const = sem("constants_written")
        CONSTS = 10
        SMALL = 4
        s_b2 = sem("b2_loaded")
        s_ident_r = sem("ident_r_written")
        s_adjf = [sem(f"adjacency_in_float{i}") for i in range(2)]
        s_adjt = sem("adjacency_transposed")
        s_adjh = sem("adjacency_high")
        s_adjl = sem("adjacency_low")
        s_gwt = sem("gnn_weights_transposed")
        s_gwh = sem("gnn_weights_high")
        s_gwl = sem("gnn_weights_low")
        s_degf = sem("degree_diagonals")
        s_degh = sem("degree_high")
        s_degl = sem("degree_low")
        s_degb = sem("degree_bias")
        s_deg = sem("degrees")
        s_big = sem("sums_of_sizes")
        s_bigp = sem("large_entries_counted")
        s_bigi = sem("large_entries_flag")
        s_b1t = sem("b1_transposed")
        s_b1 = sem("b1_columns")
        s_x = [sem(f"x_loaded{i}") for i in range(2)]
        s_bn1, s_mv1, s_ve1 = sem("bn1"), sem("mean_var1"), sem("eps_and_minus_mean1")
        s_rs1, s_sh1 = sem("inverse_std1"), sem("shift1")
        s_xn = sem("xn_written")
        s_xnh, s_xnl = sem("xn_high"), sem("xn_low")
        s_xb = sem("xb_written")
        s_agg = sem("aggregated")
        s_agh, s_agl = sem("aggregated_high"), sem("aggregated_low")
        s_fin = sem("weight_products")
        s_x1 = sem("x1_written")
        s_no = sem("token_numbers_in_x1")
        s_bn2, s_mv2, s_ve2 = sem("bn2"), sem("mean_var2"), sem("eps_and_minus_mean2")
        s_rs2, s_sh2 = sem("inverse_std2"), sem("shift2")
        s_xm = sem("xm_written")
        s_xmh, s_xml = sem("xm_high"), sem("xm_low")
        s_tr = sem("xm_transposed")
        s_xmt = sem("xm_transposed_copied")
        s_log = sem("logits")
        s_gate = sem("gate_steps")
        s_seen = sem("seen_updated")
        s_rank = sem("ranks")
        s_slot = sem("slot_steps")
        s_sc = [sem(f"rows_scattered{i}") for i in range(2)]
        s_total = sem("totals")
        s_table = sem("table_steps")
        TABLE = 4
        s_base = sem("tiles_before_steps")
        s_fill = sem("filling_stored")
        s_raw = [sem(f"expert_weights_loaded{i}") for i in range(2)]
        s_ewh, s_ewl = sem("expert_weights_high"), sem("expert_weights_low")
        s_rt = sem("row_tile_loaded")
        s_bn3, s_mv3, s_ve3 = sem("bn3"), sem("mean_var3"), sem("eps_and_minus_mean3")
        s_rs3, s_sh3 = sem("inverse_std3"), sem("shift3")
        s_zn, s_znh, s_znl = sem("zn_written"), sem("zn_high"), sem("zn_low")
        s_zt = sem("zn_transposed")
        s_zth, s_ztl = sem("zn_transposed_high"), sem("zn_transposed_low")
        s_h = sem("hidden_chunks")
        s_hr, s_hh, s_hh_act = sem("relu_chunks"), sem("hidden_high"), sem("hidden_high_by_scalar")
        s_hl, s_hl3 = sem("hidden_low"), sem("hidden_low_of_the_last_chunk")
        s_free = sem("ring_tiles_read")
        s_tok = sem("tokens_copied")
        s_yp = sem("output_products")
        s_y = sem("y_written")
        s_out = sem("output_scattered")

        s_passed = sem("waits_passed")

        def hold(engine):
            engine.sem_inc(s_passed, 1)

        def tiles_of(engine, pair):
            word = engine.value_load(pair_words[0:1, bass.ds(pair, 1)], min_val=1, max_val=FIELD ** 3 - 1)
            most = T // TILE
            tiles = [engine.snap((word % FIELD).with_bounds(min_val=1, max_val=most)),
                     engine.snap((word // FIELD % FIELD).with_bounds(min_val=1, max_val=most))]
            before = engine.snap((word // FIELD ** 2).with_bounds(min_val=0, max_val=most + E - 2))
            return [(tiles[0], before), (tiles[1], engine.snap((before + tiles[0]).with_bounds(min_val=1, max_val=most + E - 1)))]

        def load_expert(engine, e, i):
            engine.dma_start(stage[:, i, 0:W1N].rearrange("p (k n) -> p k n", k=KD),
                             w1[e].rearrange("(k p) n -> p k n", p=P)).then_inc(s_raw[i], 16)
            engine.dma_start(stage[:, i, W1N:].rearrange("p (k n) -> p k n", k=KH),
                             w2[e].rearrange("(k p) n -> p k n", p=P)).then_inc(s_raw[i], 16)

        def flat(a):
            return a.rearrange("p t e -> p (t e)")

        def nth_of_parity(b, parity, amount):
            return (b - parity) * (amount // 2) + amount

        def tr_bank(h, aggregating):
            return tr_ps[:] if aggregating or not h else agg_ps[1][:, 0, :]

        def first(s):
            return isinstance(s, int) and s == 0

        def final(b):
            return isinstance(b, int) and b == B - 1

        def x1_of(b, parity):
            return x1[2] if final(b) else x1[parity]

        def reused(b):
            return not isinstance(b, int) or b >= 2

        def later(b):
            return not isinstance(b, int) or b >= 1

        def stages(step, engine):
            begin, end = 5, B - 3
            for s in range(-1, begin):
                step(s, s % 2, lambda off, s=s: 0 <= s + off < B)
            with engine.Fori(0, (end - begin) // 2) as pair:
                for u in range(2):
                    step(2 * pair + (begin + u), (begin + u) % 2, lambda off: True)
            for s in range(end, B + 3):
                step(s, s % 2, lambda off, s=s: 0 <= s + off < B)

        block = ctx.enter_context(nc.Block())

        @block.sync
        def _(sp):
            sp.dma_start(xin[0][:], x[0].rearrange("(t p) d -> p t d", p=P)).then_inc(s_x[0], 16)
            for h in range(2):
                sp.dma_start(adj_i[:, h * HALF:(h + 1) * HALF, :],
                             adj[h * HALF * P:(h + 1) * HALF * P].rearrange("(t p) s -> p t s", p=P)).then_inc(s_adj[h], 16)
            sp.dma_start(gw_n[:], gnn_w.rearrange("(o p) n -> p o n", p=P)).then_inc(s_gw, 16)
            sp.dma_start(xin[1][:], x[1].rearrange("(t p) d -> p t d", p=P)).then_inc(s_x[1], 16)
            for i in range(2):
                n = E // 2
                sp.dma_start(b2_sb[:, i * n * D:(i + 1) * n * D],
                             b2[i * n:(i + 1) * n].rearrange("e d -> (e d)").unsqueeze(0).to_broadcast([P, n * D])).then_inc(s_b2, 16)

            sp.wait_ge(s_adjt, 1)
            sp.wait_ge(s_big, 2)
            sp.wait_ge(s_deg, 1)
            for i in range(2):
                load_expert(sp, i, i)
            with sp.Fori(1, B // 2) as pair:
                for parity in range(2):
                    b = 2 * pair + parity
                    sp.wait_ge(s_xb, 2 * (b - 1))
                    hold(sp)
                    sp.wait_ge(s_xn, NT * (b - 1))
                    hold(sp)
                    sp.dma_start(xin[parity][:], x[b].rearrange("(t p) d -> p t d", p=P)).then_inc(s_x[parity], 16)

            def fill_behind(e):
                end = sp.value_load(table_i[0:1, 0, bass.ds(e, 1)], min_val=0, max_val=E * CAP - TILE)
                sp.dma_start(rows[bass.ds(end, TILE), :].rearrange("(t p) n -> p t n", p=P),
                             filling[:]).then_inc(s_fill, 16)

            sp.wait_ge(s_table, 1)
            sp.wait_ge(s_const, CONSTS)
            fill_behind(0)
            sp.wait_ge(s_table, TABLE)

            def load_tile(g, row):
                sp.wait_ge(s_free, 2 * g + 2)
                hold(sp)
                sp.wait_ge(s_rt, 16 * (g + 1))
                hold(sp)
                sp.dma_start(rt[:, bass.ds(g % RING, 1), :, :].rearrange("p a t n -> p (a t) n"),
                             rows[bass.ds(row, TILE), :].rearrange("(t p) n -> p t n", p=P)).then_inc(s_rt, 16)

            sp.sem_inc(s_rt, 16)
            with sp.Fori(0, E // 2) as pair:
                counts = tiles_of(sp, pair)
                for i in range(2):
                    e = 2 * pair + i
                    tiles, base = counts[i]
                    sp.wait_ge(s_fill, 16 * (e + 1))
                    hold(sp)
                    for parity in range(2):
                        sp.wait_ge(s_sc[parity], 16 * NT * B // 2)
                    with sp.Fori(0, tiles) as n:
                        g = base + n
                        load_tile(g, e * CAP + n * TILE)
                    with sp.If(e < E - 1):
                        fill_behind((e + 1) % E)
            total = counts[1][0] + counts[1][1]
            for n in range(3):
                load_tile(total + n, 0)
            sp.wait_ge(s_rt, 16 * (total + 4))
            hold(sp)
            sp.wait_ge(s_out, 16 * TH * (total + 1))
            hold(sp)

        @block.tensor
        def _(pe):
            def keep_busy(n, bank=agg_ps[0][:, 0, 0:TILE], early=False):
                for _ in range(n):
                    if early:
                        pe.matmul(bank, ident[:], ident[:], start=True, stop=True)
                    else:
                        pe.matmul(bank, ident_r[:], gw_h[:, 0, :], start=True, stop=True)

            pe.wait_ge(s_ident, 1)
            for t in range(NT):
                pe.wait_ge(s_adjf[t // HALF], t % HALF + 1)
                for j in range(NT):
                    m = pe.transpose(adjt_ps[j][:, t * P:(t + 1) * P], adj_f[:, t, j * P:(j + 1) * P], ident[:])
            m.then_inc(s_adjt, 1)
            pe.wait_ge(s_gw, 16)
            for c in range(2 * KD):
                for o in range(KD):
                    m = pe.transpose(gwt_ps[:, c, o * P:(o + 1) * P], gw_n[:, o, c * P:(c + 1) * P], ident[:])
            m.then_inc(s_gwt, 1)
            pe.wait_ge(s_small, 16 * SMALL)
            pe.transpose(b1t_ps, b1_n[:], ident[0:E * KH, 0:E * KH]).then_inc(s_b1t, 1)
            keep_busy(3, agg_ps[0][:, 1, TILE:TILE + P], early=True)
            pe.wait_ge(s_big, 3)
            pe.wait_ge(s_ones, 1)
            pe.matmul(big_ps, big[:, 2:3], ones_f[:], start=True, stop=True).then_inc(s_bigp, 1)
            pe.wait_ge(s_bigi, 1)
            large = pe.value_load(big_i[0:1, 0:1], min_val=0, max_val=P)
            pe.wait_ge(s_adjh, NT + 1)
            pe.wait_ge(s_degh, 2)
            pe.wait_ge(s_zeros, 2)
            pe.wait_ge(s_b1, 1)
            keep_busy(2, agg_ps[0][:, 1, TILE:TILE + P], early=True)

            def aggregate_by(p, d, parts):
                tile3 = agg_ps[d][:, 1, :].rearrange("p (t k) -> p t k", k=P)
                for j in range(NT):
                    for q, xpart in enumerate((xn_h[p], xn_l[p])):
                        xw = xpart[:, j, d * P:(d + 1) * P]
                        for a in parts:
                            begin = (j, q, a) == (0, 0, 0)
                            end = (j, q, a) == (NT - 1, 1, parts[-1])
                            if j == 0:
                                pe.matmul(agg_ps[d][:, 0, :], xw, tile0[a][:, 0, :], start=begin, stop=end)
                                n = S if begin else P
                                pe.matmul(agg_ps[d][:, 1, 0:n], xw, tile0[a][:, 1, 0:n], start=begin, stop=end)
                            else:
                                pe.matmul(agg_ps[d][:, 0, 0:SC], xw, tiles13[a][:, j - 1, 0:SC], start=begin, stop=end)
                                m = pe.matmul(tile3[:, 0:j + 1:j, :], xw, tiles13[a][:, j - 1, SC:], start=begin, stop=end)
                m.then_inc(s_agg, 1)

            def weight_products(p, t):
                n = 0
                places = ((0, NT - 1) if t == 0 else (1, t), (0, t) if t < NT - 1 else (1, 0))
                for w, (bank, k) in enumerate(places):
                    for d in range(KD):
                        for hl, gws in ((0, (gw_h, gw_l)), (1, (gw_h,))):
                            for gw in gws:
                                m = pe.matmul(fin_ps[:, t, :], ag[p][hl][:, d, bank, k * P:(k + 1) * P],
                                              gw[:, w * KD + d, :], start=(n == 0), stop=(n == 6 * KD - 1))
                                n += 1
                m.then_inc(s_fin, 1)

            def transpose_half(h, bank):
                for t in range(HALF):
                    for d in range(KD):
                        o = (t * KD + d) * P
                        for q, part in enumerate((xm_h, xm_l)):
                            m = pe.matmul(bank[:, o:o + P], part[:, h * HALF + t, d * P:(d + 1) * P], ident_r[:],
                                          start=(q == 0), stop=(q == 1))
                m.then_inc(s_tr, 1)

            def ranks(b, q):
                pe.wait_ge(s_gate, 6 * (b + 1))
                if later(b):
                    pe.wait_ge(s_seen, 2 * b)
                r = rank_ps.rearrange("p (t e) -> p t e", t=NT)
                pe.matmul(rank_ps, before_b[:], chosen[q][:].rearrange("p t e -> p (t e)"), start=True, stop=False)
                pe.matmul(r, ones_b[:], seen[q][:].unsqueeze(1).to_broadcast([P, NT, E]), start=False, stop=False)
                for t in range(NT - 1):
                    m = pe.matmul(r[:, t + 1:, :], ones_b[:],
                                  chosen[q][:, t:t + 1, :].to_broadcast([P, NT - 1 - t, E]),
                                  start=False, stop=(t == NT - 2))
                m.then_inc(s_rank, 1)

            def aggregate(s, p, has, parts):
                aggregate_by(p, 0, parts)
                if has(-3):
                    ranks(s - 3, 1 - p)
                if first(s):
                    pe.wait_ge(s_gwl, 1)
                if later(s):
                    pe.wait_ge(s_agl, 2 * s)
                aggregate_by(p, 1, parts)

            def step(s, p, has):
                q = 1 - p
                alone = has(-2) and not has(-1)
                if has(0):
                    pe.wait_ge(s_xnl, s + 1)
                    if later(s):
                        pe.wait_ge(s_agl, 2 * s - 1)
                    hold(pe)
                    with pe.If(large > 0):
                        pe.wait_ge(s_adjl, NT + 1)
                        pe.wait_ge(s_degl, 2)
                        aggregate(s, p, has, [0, 1])
                    with pe.Else():
                        aggregate(s, p, has, [0])
                elif has(-3) and not has(-1):
                    if alone:
                        keep_busy(10)
                    ranks(s - 3, q)
                    if alone:
                        keep_busy(12)
                for t in range(NT):
                    if has(-1):
                        b = s - 1
                        if first(b) and t == 0:
                            pe.wait_ge(s_adjl, NT + 1)
                        if t == 0:
                            pe.wait_ge(s_agl, 2 * (b + 1))
                        if t % HALF == 0 and later(b):
                            pe.wait_ge(s_x1, 2 * b - 1 + t // HALF)
                        weight_products(q, t)
                    if has(-3) and has(-1) and not has(0) and t == 0:
                        ranks(s - 3, q)
                    halves = [h for h in range(2) if t == (h if has(0) else NT - 1)]
                    for h in halves if has(-2) else []:
                        b = s - 2
                        if first(b):
                            pe.wait_ge(s_ident_r, 1)
                            pe.wait_ge(s_const, CONSTS)
                            if h == 0:
                                keep_busy(32, misc_ps[:, TILE:])
                        pe.wait_ge(s_xml, 2 * b + h + 1)
                        if (h and has(0)) or later(b):
                            pe.wait_ge(s_xmt, 2 * b + (h if has(0) else 0))
                        transpose_half(h, tr_bank(h, has(0)))
                        if alone:
                            keep_busy(6 - 3 * h)
                    if has(-2) and t == NT - 1:
                        b = s - 2
                        if later(b):
                            pe.wait_ge(s_slot, 4 * b)
                        for u in range(NT):
                            if u % HALF == 0:
                                pe.wait_ge(s_xmt, 2 * b + u // HALF + 1)
                            for d in range(KD):
                                o = (u % HALF * KD + d) * P
                                m = pe.matmul(logit_ps[:, u * E:(u + 1) * E], xm_t[:, u // HALF, o:o + P], wg_sb[:, d, :],
                                              start=(d == 0), stop=(d == KD - 1))
                        m.then_inc(s_log, 1)

            stages(step, pe)

            pe.wait_ge(s_seen, 2 * B)
            pe.wait_ge(s_slot, 4 * B)
            pe.matmul(total_ps, ones_b[:], seen[B % 2][:], start=True, stop=True).then_inc(s_total, 1)

            pe.wait_ge(s_table, TABLE)

            def transpose_rows(g):
                pe.wait_ge(s_znl, g + 1)
                for bank, part in ((th_ps, zn_h), (tl_ps, zn_l)):
                    for t in range(TH):
                        for d in range(KD):
                            o = d * TILE + t * P
                            m = pe.matmul(bank[:, o:o + P], part[:, t, d * P:(d + 1) * P], ident_r[:],
                                          start=True, stop=True)
                m.then_inc(s_zt, 1)

            def ffn(g, e, i):
                pe.wait_ge(s_zth, g + 1)
                for c in range(KH):
                    for n, (w, zt) in enumerate(((w1_h[i], zt_h), (w1_l[i], zt_h), (w1_h[i], zt_l))):
                        if c == 0 and n == 2:
                            pe.wait_ge(s_ztl, g + 1)
                        for d in range(KD):
                            m = pe.matmul(h_ps[c], w[:, d, c * P:(c + 1) * P], zt[:, d, :],
                                          start=(n == 0 and d == 0), stop=(n == 2 and d == KD - 1))
                    m.then_inc(s_h, 1)
                pe.wait_ge(s_ewl, QUARTERS * (e + 1))
                hold(pe)
                pe.wait_ge(s_y, TH * (g + 1))
                for c in range(KH):
                    if c == HALF_H:
                        transpose_rows(g + 1)
                    if c < KH - 1:
                        pe.wait_ge(s_hl, (KH - 1) * g + c + 1)
                    else:
                        pe.wait_ge(s_hl3, g + 1)
                    for t in range(TH):
                        for hid, ws in ((hh, (w2_h[i], w2_l[i])), (hl_, (w2_h[i],))):
                            for k, w in enumerate(ws):
                                m = pe.matmul(y_ps[t], hid[:, c, t * P:(t + 1) * P], w[:, c, :],
                                              start=(c == 0 and hid is hh and k == 0), stop=(c == KH - 1 and hid is hl_))
                        if c == KH - 1:
                            m.then_inc(s_yp, 1)

            pe.wait_ge(s_rt, 32)
            keep_busy(22)
            transpose_rows(0)
            with pe.Fori(0, E // 2) as pair:
                counts = tiles_of(pe, pair)
                for i in range(2):
                    e = 2 * pair + i
                    tiles, base = counts[i]
                    pe.wait_ge(s_ewl, QUARTERS * e + QUARTERS // 2)
                    hold(pe)
                    with pe.Fori(0, tiles) as n:
                        ffn(base + n, e, i)

        @block.scalar
        def _(act):
            act.dma_start(gb[:], gnn_b.unsqueeze(0).to_broadcast([P, D])).then_inc(s_small, 16)
            act.dma_start(b1_n[:], b1.rearrange("e (k p) -> (e k) p", p=P)).then_inc(s_small, 16)
            with nc.allow_non_contiguous_dma(reason="eight columns"):
                act.dma_start(wg_sb[:], wg.rearrange("(k p) e -> p k e", p=P)).then_inc(s_small, 16)
            act.dma_start(bg_sb[:], bg.unsqueeze(0).to_broadcast([P, E])).then_inc(s_small, 16)
            for t in range(HALF):
                act.wait_ge(s_adj[0], 16)
                act.activation(adj_f[:, t, :], adj_i[:, t, :], ACT.Copy, accum_out=deg[:, t:t + 1]).then_inc(s_adjf[0], 1)

            def setup():
                act.wait_ge(s_adjt, 1)
                act.activation(tile0[0][:, 0, 0:SC], adjt_ps[0][:, 0:SC], ACT.Copy).then_inc(s_adjh, 1)
                act.activation(tile0[0][:, 1, 0:P], adjt_ps[0][:, SC:], ACT.Copy).then_inc(s_adjh, 1)
                act.activation(tiles13[0][:, 0, 0:S], adjt_ps[1], ACT.Copy).then_inc(s_adjh, 1)
                act.wait_ge(s_degf, NT)
                act.activation(tile0[0][:, 0, SC:], deg_f[:, 0, :], ACT.Copy).then_inc(s_degh, 1)
                act.activation(tiles13[0][:, :, S:], deg_f[:, 1:, :], ACT.Copy).then_inc(s_degh, 1)
                act.wait_ge(s_b1t, 1)
                act.activation(b1_t[:], b1t_ps, ACT.Copy).then_inc(s_b1, 1)
                act.wait_ge(s_gwt, 1)
                act.activation(gw_h[:], gwt_ps, ACT.Copy).then_inc(s_gwh, 1)
                act.wait_ge(s_ident, 1)
                act.activation(ident_r[:], ident[:], ACT.Copy).then_inc(s_ident_r, 1)

            def step(s, p, has):
                q = 1 - p
                if first(s):
                    setup()
                if has(1):
                    b = s + 1
                    act.wait_ge(s_sh1, b + 1)
                    if later(b):
                        act.wait_ge(s_xnl, b)
                        act.wait_ge(s_xnh, b)
                    for t in range(NT):
                        act.activation(xn[:, t, :], xin[q][:, t, :], ACT.Identity, scale=rs1[:, t:t + 1],
                                       bias=sh1[:, t:t + 1]).then_inc(s_xn, 1)
                    act.wait_ge(s_xn, NT * (b + 1))
                    if reused(b):
                        act.wait_ge(s_agg, 2 * (b - 1))
                    act.activation(xn_h[q][:], xn[:], ACT.Copy).then_inc(s_xnh, 1)
                if has(0):
                    act.wait_ge(s_agg, 2 * s + 1)
                    if reused(s):
                        act.wait_ge(s_fin, NT * (s - 1))
                    act.activation(ag[p][0][:, 0], agg_ps[0][:], ACT.Copy).then_inc(s_agh, 1)
                if has(-2):
                    b = s - 2
                    act.wait_ge(s_sh2, b + 1)
                    for h in range(2):
                        ts = slice(h * HALF, (h + 1) * HALF)
                        if later(b):
                            act.wait_ge(s_xml, 2 * b)
                            act.wait_ge(s_xmh, 2 * b)
                        for t in range(h * HALF, (h + 1) * HALF):
                            act.activation(xm[:, t, :], x1_of(b, p)[:, t, 0:D], ACT.Identity, scale=rs2[:, t:t + 1],
                                           bias=sh2[:, t:t + 1]).then_inc(s_xm, 1)
                        act.wait_ge(s_xm, NT * b + HALF * (h + 1))
                        if later(b):
                            act.wait_ge(s_tr, 2 * b)
                        act.activation(xm_h[:, ts, :], xm[:, ts, :], ACT.Copy).then_inc(s_xmh, 1)
                for h in range(2):
                    if has(-2):
                        b = s - 2
                        act.wait_ge(s_tr, 2 * b + h + 1)
                        if later(b):
                            act.wait_ge(s_log, b)
                        act.activation(xm_t[:, h, :], tr_bank(h, has(0)), ACT.Copy).then_inc(s_xmt, 1)
                    if h == 0 and has(0):
                        act.wait_ge(s_agg, 2 * s + 2)
                        act.activation(ag[p][0][:, 1], agg_ps[1][:], ACT.Copy).then_inc(s_agh, 1)

            stages(step, act)

            act.wait_ge(s_table, TABLE)

            def split_quarter(e, i, k, tiles_done):
                act.wait_ge(s_raw[i], nth_of_parity(e, i, 32))
                if tiles_done is None:
                    act.wait_ge(s_fin, NT * B)
                else:
                    act.wait_ge(s_y, TH * (tiles_done + 1))
                act.activation(ew_h[i][:, bass.ds(k % QUARTERS * QN, QN)], stage[:, i, bass.ds(k % QUARTERS * QN, QN)], ACT.Copy).then_inc(s_ewh, 1)

            def normalise(g):
                act.wait_ge(s_sh3, g + 1)
                if later(g):
                    act.wait_ge(s_znl, g)
                    act.wait_ge(s_znh, g)
                for t in range(TH):
                    act.activation(zn[:, t, :], rt[:, bass.ds(g % RING, 1), t, 0:D].rearrange("p a d -> p (a d)"), ACT.Identity, scale=rs3[:, t:t + 1],
                                   bias=sh3[:, t:t + 1]).then_inc(s_zn, 1)

            def high_rows(g):
                act.wait_ge(s_zn, TH * (g + 1))
                if later(g):
                    act.wait_ge(s_zt, g)
                act.activation(zn_h[:], zn[:], ACT.Copy).then_inc(s_znh, 1)

            def copy_transposed(g):
                act.wait_ge(s_zt, g + 1)
                act.activation(zt_h[:].rearrange("p k n -> p (k n)"), th_ps[:], ACT.Copy).then_inc(s_zth, 1)

            for k in range(QUARTERS):
                split_quarter(0, 0, k, None)
            normalise(0)
            high_rows(0)
            normalise(1)
            copy_transposed(0)
            high_rows(1)
            with act.Fori(0, E // 2) as pair:
                counts = tiles_of(act, pair)
                for i in range(2):
                    e = 2 * pair + i
                    tiles, base = counts[i]
                    more = QUARTERS * ((e + 1) // E) if i else 0
                    with act.Fori(0, tiles) as n:
                        g = base + n
                        for c in range(KH):
                            act.wait_ge(s_h, KH * g + c + 1)
                            act.activation(hr[:, c, :], h_ps[c], ACT.Relu,
                                           bias=b1_t[:, bass.ds(e * KH + c, 1)]).then_inc(s_hr, 1)
                            if c < HALF_H:
                                act.activation(hh[:, c, :], h_ps[c], ACT.Relu,
                                               bias=b1_t[:, bass.ds(e * KH + c, 1)]).then_inc(s_hh_act, 1)
                        normalise(g + 2)
                        with act.If(n + more < QUARTERS):
                            split_quarter(e + 1, 1 - i, n, base)
                            with act.If(n + e // (E - 2) < 1):
                                act.wait_ge(s_ewl, QUARTERS * (e + 1))
                                hold(act)
                                load_expert(act, (e + 2) % E, i)
                        copy_transposed(g + 1)
                        high_rows(g + 2)
                    with act.If(tiles + more < QUARTERS):
                        for k in range(1, QUARTERS):
                            with act.If(tiles <= k):
                                split_quarter(e + 1, 1 - i, k, base)

        @block.vector
        def _(dve):
            def low_adjacency():
                def low(part, whole):
                    high = part[0].bitcast(F32)
                    return dve.tensor_tensor(part[1], whole, high, ALU.subtract)

                def both(pair, *index):
                    return [part[index] for part in pair]

                dve.wait_ge(s_adjh, NT + 1)
                every = slice(None)
                low(both(tile0, every, 0, slice(0, SC)), adjt_ps[0][:, 0:SC]).then_inc(s_adjl, 1)
                low(both(tile0, every, 1, slice(0, P)), adjt_ps[0][:, SC:]).then_inc(s_adjl, 1)
                for j in range(1, NT):
                    low(both(tiles13, every, j - 1, slice(0, S)), adjt_ps[j]).then_inc(s_adjl, 1)
                dve.wait_ge(s_degh, 2)
                dve.wait_ge(s_degf, NT)
                low(both(tile0, every, 0, slice(SC, S)), deg_f[:, 0, :]).then_inc(s_degl, 1)
                low(both(tiles13, every, every, slice(S, S + P)), deg_f[:, 1:, :]).then_inc(s_degl, 1)

            def sum_of_sizes(h):
                dve.wait_ge(s_adj[h], 16)
                dve.tensor_reduce(big[:, h:h + 1], adj_i[:, h * HALF:(h + 1) * HALF, :].rearrange("p t s -> p (t s)").bitcast(U32),
                                  AX_X, ALU.add).then_inc(s_big, 1)

            def tile_statistics1(b, p, tiles):
                dve.wait_ge(s_x[p], nth_of_parity(b, p, 16))
                if later(b):
                    dve.wait_ge(s_ve1, 2 * b)
                    dve.wait_ge(s_mv1, NT * b)
                for t in tiles:
                    dve.bn_stats(st1[:, t, :], xin[p][:, t, :]).then_inc(s_bn1, 1)

            def aggregate_statistics1(b):
                dve.wait_ge(s_bn1, NT * (b + 1))
                hold(dve)
                for t in range(NT):
                    dve.bn_aggr(mv1[:, t, :], st1[:, t, :]).then_inc(s_mv1, 1)
                dve.wait_ge(s_mv1, NT * (b + 1))
                if later(b):
                    dve.wait_ge(s_sh1, b)
                dve.tensor_scalar(ve1[:], mv1[:, :, 1], EPS, None, ALU.add).then_inc(s_ve1, 1)
                dve.tensor_scalar(nm1[:], mv1[:, :, 0], -1.0, None, ALU.mult).then_inc(s_ve1, 1)

            def statistics1(b, p):
                tile_statistics1(b, p, range(NT))
                aggregate_statistics1(b)

            def low_aggregate(s, p, d):
                dve.wait_ge(s_agh, 2 * s + d + 1)
                dve.tensor_tensor(ag[p][1][:, d], agg_ps[d][:], ag[p][0][:, d].bitcast(F32),
                                  ALU.subtract).then_inc(s_agl, 1)

            def add_x1(b, q, h):
                ts = slice(h * HALF, (h + 1) * HALF)
                dve.wait_ge(s_fin, NT * b + HALF * (h + 1))
                dve.tensor_tensor(x1_of(b, q)[:, ts, 0:D], fin_ps[:, ts, :], xb[q][:, ts, :], ALU.add).then_inc(s_x1, 1)
                dve.wait_ge(s_x1, 2 * b + h + 1)

            def choose(b, p):
                g = 6 * b
                dve.wait_ge(s_log, b + 1)
                if later(b):
                    dve.wait_ge(s_gate, g)
                dve.tensor_tensor(logit[:], logit_ps.rearrange("p (t e) -> p t e", t=NT),
                                  bg_sb[:].unsqueeze(1).to_broadcast([P, NT, E]), ALU.add).then_inc(s_gate, 1)
                dve.wait_ge(s_gate, g + 1)
                dve.tensor_reduce(top[:], logit[:], AX_X, ALU.max).then_inc(s_gate, 1)
                dve.wait_ge(s_gate, g + 2)
                dve.tensor_tensor(score[:], logit[:], top[:].unsqueeze(2).to_broadcast([P, NT, E]),
                                  ALU.is_equal).then_inc(s_gate, 1)
                dve.wait_ge(s_gate, g + 3)
                dve.tensor_tensor(score[:], score[:], order[:], ALU.mult).then_inc(s_gate, 1)
                dve.wait_ge(s_gate, g + 4)
                dve.tensor_reduce(best[:], score[:], AX_X, ALU.max).then_inc(s_gate, 1)
                dve.wait_ge(s_gate, g + 5)
                if reused(b):
                    dve.wait_ge(s_slot, 4 * (b - 1))
                    dve.wait_ge(s_rank, b - 1)
                    dve.wait_ge(s_seen, 2 * (b - 1))
                dve.tensor_tensor(chosen[p][:], score[:], best[:].unsqueeze(2).to_broadcast([P, NT, E]),
                                  ALU.is_equal).then_inc(s_gate, 1)

            def step(s, p, has):
                q = 1 - p
                if first(s):
                    low_adjacency()
                if has(-3):
                    b = s - 3
                    dve.wait_ge(s_rank, b + 1)
                    if later(b):
                        dve.wait_ge(s_slot, 4 * b)
                    dve.tensor_tensor(flat(place[:]), rank_ps, flat(region[:]), ALU.add).then_inc(s_slot, 1)
                    dve.wait_ge(s_slot, 4 * b + 1)
                    dve.tensor_tensor(place[:], place[:], chosen[q][:], ALU.mult).then_inc(s_slot, 1)
                    dve.wait_ge(s_slot, 4 * b + 2)
                    dve.tensor_reduce(slot[:], place[:], AX_X, ALU.add).then_inc(s_slot, 1)
                    dve.wait_ge(s_slot, 4 * b + 3)
                    if reused(b):
                        dve.wait_ge(s_sc[q], nth_of_parity(b - 2, q, 16 * NT))
                    dve.tensor_copy(slot_i[q][:], slot[:]).then_inc(s_slot, 1)
                if has(0):
                    if reused(s):
                        dve.wait_ge(s_fin, NT * (s - 1))
                    low_aggregate(s, p, 0)
                if has(-2):
                    b = s - 2
                    for h in range(2):
                        ts = slice(h * HALF, (h + 1) * HALF)
                        dve.wait_ge(s_xmh, 2 * b + h + 1)
                        if later(b):
                            dve.wait_ge(s_tr, 2 * b)
                        dve.tensor_tensor(xm_l[:, ts, :], xm[:, ts, :], xm_h[:, ts, :].bitcast(F32),
                                          ALU.subtract).then_inc(s_xml, 1)
                        if h == 0 and has(2):
                            tile_statistics1(s + 2, p, range(NT - 1))
                if has(2) and has(0):
                    tile_statistics1(s + 2, p, [NT - 1] if has(-2) else range(NT))
                    aggregate_statistics1(s + 2)
                if has(0):
                    low_aggregate(s, p, 1)
                if has(-1):
                    b = s - 1
                    dve.wait_ge(s_xb, 2 * (b + 1))
                    if reused(b) and not final(b):
                        dve.wait_ge(s_sc[q], nth_of_parity(b - 2, q, 16 * NT))
                        dve.wait_ge(s_xm, NT * (b - 1))
                    add_x1(b, q, 0)
                    if later(b):
                        dve.wait_ge(s_mv2, NT * b)
                    for t in range(HALF):
                        dve.bn_stats(st2[:, t, :], x1_of(b, q)[:, t, 0:D]).then_inc(s_bn2, 1)
                if has(-1):
                    b = s - 1
                    add_x1(b, q, 1)
                    for t in range(HALF, NT):
                        dve.bn_stats(st2[:, t, :], x1_of(b, q)[:, t, 0:D]).then_inc(s_bn2, 1)
                    dve.wait_ge(s_bn2, NT * (b + 1))
                    if later(b):
                        dve.wait_ge(s_ve2, 2 * b)
                    hold(dve)
                    for t in range(NT):
                        dve.bn_aggr(mv2[:, t, :], st2[:, t, :]).then_inc(s_mv2, 1)
                    dve.wait_ge(s_mv2, NT * (b + 1))
                    if later(b):
                        dve.wait_ge(s_sh2, b)
                    dve.tensor_scalar(ve2[:], mv2[:, :, 1], EPS, None, ALU.add).then_inc(s_ve2, 1)
                    dve.tensor_scalar(nm2[:], mv2[:, :, 0], -1.0, None, ALU.mult).then_inc(s_ve2, 1)
                    dve.tensor_copy(x1_of(b, q)[:, :, D:D + 1].bitcast(I32),
                                    token_no[:, bass.ds(b * NT, NT)].unsqueeze(2)).then_inc(s_no, 1)
                if has(-2):
                    b = s - 2
                    choose(b, p)
                    dve.wait_ge(s_gate, 6 * (b + 1))
                    if later(b):
                        dve.wait_ge(s_seen, 2 * b)
                    dve.tensor_reduce(added[:], chosen[p][:].rearrange("p t e -> p e t"), AX_X,
                                      ALU.add).then_inc(s_seen, 1)
                    dve.wait_ge(s_seen, 2 * b + 1)
                    if later(b):
                        dve.wait_ge(s_rank, b)
                    dve.tensor_tensor(seen[q][:], seen[p][:], added[:], ALU.add).then_inc(s_seen, 1)

            statistics1(0, 0)
            sum_of_sizes(0)
            dve.wait_ge(s_adj[1], 16)
            for t in range(HALF, NT):
                dve.tensor_copy(adj_f[:, t, :], adj_i[:, t, :]).then_inc(s_adjf[1], 1)
            dve.wait_ge(s_adjf[1], HALF)
            dve.tensor_reduce(deg[:, HALF:], adj_f[:, HALF:, :], AX_X, ALU.add).then_inc(s_deg, 1)
            dve.wait_ge(s_ident, 1)
            dve.wait_ge(s_adjf[0], HALF)
            dve.wait_ge(s_deg, 1)
            for t in range(NT):
                dve.tensor_scalar(deg_f[:, t, :], ident[:], deg[:, t:t + 1], None, ALU.mult).then_inc(s_degf, 1)
            sum_of_sizes(1)
            dve.wait_ge(s_big, 2)
            dve.tensor_scalar(big[:, 2:3], big[:, 0:1], big[:, 1:2], EXACT, ALU.add, ALU.is_gt).then_inc(s_big, 1)
            for j in range(HALF, NT):
                dve.wait_ge(s_adjt, 1)
                dve.tensor_copy(tiles13[0][:, j - 1, 0:S], adjt_ps[j]).then_inc(s_adjh, 1)
            dve.wait_ge(s_bigp, 1)
            dve.tensor_copy(big_i[:], big_ps).then_inc(s_bigi, 1)
            statistics1(1, 1)
            dve.wait_ge(s_gwh, 1)
            dve.tensor_tensor(gw_l[:], gwt_ps, gw_h[:].bitcast(F32), ALU.subtract).then_inc(s_gwl, 1)
            dve.wait_ge(s_small, 16 * SMALL)
            for t in range(NT):
                dve.tensor_scalar(deg_b[:, t, :], gb[:], deg[:, t:t + 1], None, ALU.mult).then_inc(s_degb, 1)
            dve.wait_ge(s_const, CONSTS)
            stages(step, dve)

            dve.wait_ge(s_total, 1)
            dve.tensor_tensor(table_i[:, 0, :], total_ps, region[:, 0, :], ALU.add).then_inc(s_table, 1)
            dve.tensor_scalar(table_i[:, 1, :], total_ps, 1.0, 0.0, ALU.subtract, ALU.max).then_inc(s_table, 1)
            dve.wait_ge(s_table, 2)
            shift = TILE.bit_length() - 1
            dve.tensor_scalar(table_i[:, 2, :], table_i[:, 1, :], shift, None, ALU.logical_shift_right).then_inc(s_table, 1)
            dve.wait_ge(s_table, 3)
            dve.tensor_scalar(table_f[:, 0, :], table_i[:, 2, :], 1.0, None, ALU.add).then_inc(s_base, 1)
            dve.wait_ge(s_base, 1)
            dve.tensor_tensor(tiles_earlier[:], earlier[:], table_f[:, 0:1, :].to_broadcast([P, E, E]), ALU.mult).then_inc(s_base, 1)
            tiles = table_f[:, 0, :].rearrange("p (n i) -> p n i", i=2)
            dve.scalar_tensor_tensor(pair_f[:], tiles[:, :, 1], float(FIELD), tiles[:, :, 0], ALU.mult, ALU.add).then_inc(s_base, 1)
            dve.wait_ge(s_base, 3)
            dve.tensor_reduce(table_f[:, 1, :], tiles_earlier[:], AX_X, ALU.add).then_inc(s_base, 1)
            dve.wait_ge(s_base, 4)
            before = table_f[:, 1, :].rearrange("p (n i) -> p n i", i=2)
            dve.scalar_tensor_tensor(pair_words[:], before[:, :, 0], float(FIELD ** 2), pair_f[:], ALU.mult, ALU.add).then_inc(s_table, 1)
            dve.wait_ge(s_table, TABLE)

            def split_quarter(e, i, k):
                dve.wait_ge(s_ewh, QUARTERS * e + k + 1)
                dve.tensor_tensor(ew_l[i][:, bass.ds(k % QUARTERS * QN, QN)], stage[:, i, bass.ds(k % QUARTERS * QN, QN)],
                                  ew_h[i][:, bass.ds(k % QUARTERS * QN, QN)].bitcast(F32), ALU.subtract).then_inc(s_ewl, 1)

            def statistics3(g):
                dve.wait_ge(s_rt, 16 * (g + 2))
                if later(g):
                    dve.wait_ge(s_mv3, TH * g)
                for t in range(TH):
                    dve.bn_stats(st3[:, t, :], rt[:, bass.ds(g % RING, 1), t, 0:D].rearrange("p a d -> p (a d)")).then_inc(s_bn3, 1)
                dve.wait_ge(s_bn3, TH * (g + 1))
                if later(g):
                    dve.wait_ge(s_ve3, 2 * g)
                hold(dve)
                for t in range(TH):
                    dve.bn_aggr(mv3[:, t, :], st3[:, t, :]).then_inc(s_mv3, 1)
                dve.wait_ge(s_mv3, TH * (g + 1))
                if later(g):
                    dve.wait_ge(s_sh3, g)
                dve.tensor_scalar(ve3[:], mv3[:, :, 1], EPS, None, ALU.add).then_inc(s_ve3, 1)
                dve.tensor_scalar(nm3[:], mv3[:, :, 0], -1.0, None, ALU.mult).then_inc(s_ve3, 1)

            def low_rows(g):
                dve.wait_ge(s_znh, g + 1)
                if later(g):
                    dve.wait_ge(s_zt, g)
                dve.tensor_tensor(zn_l[:], zn[:], zn_h[:].bitcast(F32), ALU.subtract).then_inc(s_znl, 1)

            def copy_transposed(g):
                dve.wait_ge(s_zt, g + 1)
                dve.tensor_copy(zt_l[:].rearrange("p k n -> p (k n)"), tl_ps[:]).then_inc(s_ztl, 1)

            dve.sem_inc(s_y, TH)
            for k in range(QUARTERS):
                split_quarter(0, 0, k)
            statistics3(0)
            statistics3(1)
            low_rows(0)
            statistics3(2)
            copy_transposed(0)
            low_rows(1)
            with dve.Fori(0, E // 2) as pair:
                counts = tiles_of(dve, pair)
                for i in range(2):
                    e = 2 * pair + i
                    tiles, base = counts[i]
                    more = QUARTERS * ((e + 1) // E) if i else 0
                    with dve.Fori(0, tiles) as n:
                        g = base + n
                        for c in range(KH):
                            dve.wait_ge(s_hr, KH * g + c + 1)
                            if c < HALF_H:
                                dve.wait_ge(s_hh_act, HALF_H * g + c + 1)
                            else:
                                dve.tensor_copy(hh[:, c, :], hr[:, c, :]).then_inc(s_hh, 1)
                            if c < KH - 1:
                                if c >= HALF_H:
                                    dve.wait_ge(s_hh, (KH - HALF_H) * g + c - HALF_H + 1)
                                dve.tensor_tensor(hl_[:, c, :], hr[:, c, :], hh[:, c, :].bitcast(F32),
                                                  ALU.subtract).then_inc(s_hl, 1)
                        statistics3(g + 3)
                        copy_transposed(g + 1)
                        with dve.If(n + more < QUARTERS):
                            split_quarter(e + 1, 1 - i, n)
                        dve.wait_ge(s_out, 16 * TH * (g + 1))
                        dve.wait_ge(s_free, 2 * (g + 1 + RING))
                        dve.tensor_copy(tok[:], tok_early[:]).then_inc(s_tok, 1)
                        for t in range(TH):
                            dve.wait_ge(s_yp, TH * g + t + 1)
                            dve.tensor_tensor(y[:, t, :], y_ps[t], res[:, t, :], ALU.add).then_inc(s_y, 1)
                        low_rows(g + 2)
                    with dve.If(tiles + more < QUARTERS):
                        for k in range(1, QUARTERS):
                            with dve.If(tiles <= k):
                                split_quarter(e + 1, 1 - i, k)

        @block.gpsimd
        def _(pool):
            pool.memset(ident[:], 0.0).then_inc(s_zero, 1)
            pool.wait_ge(s_zero, 1)
            pool.affine_select(out=ident[:], in_=ident[:], compare_op=ALU.not_equal, fill=1.0, base=0,
                               pattern=[[-1, P]], channel_multiplier=1).then_inc(s_ident, 1)
            pool.memset(ones_f[:], 1.0).then_inc(s_ones, 1)
            pool.memset(minus_half[:], -0.5).then_inc(s_half, 1)

            def shift(ve, nm, rs, sh, s_rs, s_sh, b, n):
                pool.tensor_tensor(rs[:], ve[:], minus_half[:, 0:n], ALU.pow).then_inc(s_rs, 1)
                pool.wait_ge(s_rs, b + 1)
                pool.tensor_tensor(sh[:], nm[:], rs[:], ALU.mult).then_inc(s_sh, 1)

            def shift1(b):
                pool.wait_ge(s_ve1, 2 * (b + 1))
                if later(b):
                    pool.wait_ge(s_xn, NT * b)
                shift(ve1, nm1, rs1, sh1, s_rs1, s_sh1, b, NT)

            for part in tile0:
                pool.memset(part[:, 1, P:].bitcast(F32), 0.0).then_inc(s_zeros, 1)
            pool.memset(ones_b[:], 1.0).then_inc(s_zero, 1)
            pool.memset(before_b[:], 1.0).then_inc(s_zero, 1)
            pool.memset(filling[:], 0.0).then_inc(s_zero, 1)
            pool.iota(region_i[:], [[0, NT], [CAP, E]], base=0, channel_multiplier=0).then_inc(s_zero, 1)
            pool.iota(order_i[:], [[0, NT], [-1, E]], base=E, channel_multiplier=0).then_inc(s_zero, 1)
            pool.memset(earlier[:], 1.0).then_inc(s_zero, 1)
            pool.wait_ge(s_zero, 7)
            pool.affine_select(out=earlier[:], in_=earlier[:], compare_op=ALU.is_gt, fill=0.0, base=0,
                               pattern=[[1, E], [-1, E]], channel_multiplier=0).then_inc(s_const, 1)
            pool.affine_select(out=before_b[:], in_=before_b[:], compare_op=ALU.is_gt, fill=0.0, base=0,
                               pattern=[[1, P]], channel_multiplier=-1).then_inc(s_const, 1)
            pool.memset(filling[:, :, D:D + 1].bitcast(I32), NO_TOKEN).then_inc(s_const, 1)
            pool.tensor_copy(region[:], region_i[:]).then_inc(s_const, 1)
            pool.tensor_copy(order[:], order_i[:]).then_inc(s_const, 1)
            pool.iota(token_no[:], [[P, T // P]], base=0, channel_multiplier=1).then_inc(s_const, 1)
            pool.memset(seen[0][:], 0.0).then_inc(s_const, 1)
            for i in range(3):
                pool.memset(x1[i][:, :, D:], 0.0).then_inc(s_const, 1)
            pool.wait_ge(s_half, 1)
            shift1(0)

            def step(s, p, has):
                q = 1 - p
                if first(s):
                    pool.wait_ge(s_degb, NT)
                if has(0):
                    pool.wait_ge(s_x[p], nth_of_parity(s, p, 16))
                    for h in range(2):
                        ts = slice(h * HALF, (h + 1) * HALF)
                        if reused(s):
                            pool.wait_ge(s_x1, 2 * (s - 2) + h + 1)
                        pool.tensor_tensor(xb[p][:, ts, :], xin[p][:, ts, :], deg_b[:, ts, :], ALU.add).then_inc(s_xb, 1)
                if has(-2):
                    b = s - 2
                    pool.wait_ge(s_ve2, 2 * (b + 1))
                    if later(b):
                        pool.wait_ge(s_xm, NT * b)
                    shift(ve2, nm2, rs2, sh2, s_rs2, s_sh2, b, NT)
                if has(-3):
                    pool.wait_ge(s_slot, 4 * (s - 3 + 1))
                    pool.wait_ge(s_no, s - 3 + 1)
                    hold(pool)
                    for t in range(NT):
                        pool.indirect_dma_start(out=rows, out_offset=bass.IndirectOffsetOnAxis(ap=slot_i[q][:, t:t + 1].bitcast(U32), axis=0),
                                                in_=x1_of(s - 3, q)[:, t, :], in_offset=None, bounds_check=E * CAP - 1,
                                                oob_is_err=False).then_inc(s_sc[q], 16)
                if has(1):
                    b = s + 1
                    pool.wait_ge(s_xnh, b + 1)
                    if reused(b):
                        pool.wait_ge(s_agg, 2 * (b - 1))
                    pool.tensor_tensor(xn_l[q][:], xn[:], xn_h[q][:].bitcast(F32), ALU.subtract).then_inc(s_xnl, 1)
                if has(2):
                    shift1(s + 2)

            stages(step, pool)

            pool.wait_ge(s_table, TABLE)
            pool.wait_ge(s_b2, 32)
            pool.sem_inc(s_free, 2 * RING)
            pool.sem_inc(s_tok, 1)

            def scatter_out(values, tokens):
                pool.indirect_dma_start(out=out_rows, out_offset=bass.IndirectOffsetOnAxis(ap=tokens.bitcast(U32), axis=0),
                                        in_=values, in_offset=None, bounds_check=T - 1,
                                        oob_is_err=False).then_inc(s_out, 16)

            for t in range(TH):
                scatter_out(filling[:, t, 0:D], filling[:, t, D:D + 1])

            def shift3(g):
                pool.wait_ge(s_ve3, 2 * (g + 1))
                if later(g):
                    pool.wait_ge(s_zn, TH * g)
                shift(ve3, nm3, rs3, sh3, s_rs3, s_sh3, g, TH)

            shift3(0)
            shift3(1)
            shift3(2)
            with pool.Fori(0, E // 2) as pair:
                counts = tiles_of(pool, pair)
                for i in range(2):
                    e = 2 * pair + i
                    tiles, base = counts[i]
                    with pool.Fori(0, tiles) as n:
                        g = base + n
                        pool.wait_ge(s_hh, (KH - HALF_H) * (g + 1))
                        pool.tensor_tensor(hl_[:, KH - 1, :], hr[:, KH - 1, :], hh[:, KH - 1, :].bitcast(F32),
                                           ALU.subtract).then_inc(s_hl3, 1)
                        pool.wait_ge(s_rt, 16 * (g + 2))
                        pool.wait_ge(s_y, TH * (g + 1))
                        hold(pool)
                        pool.tensor_tensor(res[:], rt[:, bass.ds(g % RING, 1), :, 0:D].rearrange("p a t d -> p (a t) d"),
                                           b2_sb[:, bass.ds(e * D, D)].unsqueeze(1).to_broadcast([P, TH, D]),
                                           ALU.add).then_inc(s_free, 1)
                        pool.wait_ge(s_tok, g + 1)
                        hold(pool)
                        pool.tensor_copy(tok_early[:].unsqueeze(2), rt[:, bass.ds(g % RING, 1), :, D:D + 1].rearrange("p a t d -> p (a t) d").bitcast(I32)).then_inc(s_free, 1)
                        shift3(g + 3)
                        pool.wait_ge(s_tok, g + 2)
                        for t in range(TH):
                            pool.wait_ge(s_y, TH * (g + 1) + t + 1)
                            hold(pool)
                            scatter_out(y[:, t, :], tok[:, t:t + 1])


def kernel(**inputs):
    import numpy as np
    import concourse.bacc as bacc
    from concourse.bass_utils import run_bass_kernel_spmd

    names = ["x", "adj", "L0_gnn_W", "L0_gnn_b", "L0_ffn_W1", "L0_ffn_b1", "L0_ffn_W2", "L0_ffn_b2", "L0_ffn_Wg", "L0_ffn_bg"]
    nc = bacc.Bacc("TRN2", target_bir_lowering=False, num_devices=1)
    arrays, args = {}, []
    for name in names:
        a = np.ascontiguousarray(inputs[name])
        arrays[name] = a
        args.append(nc.dram_tensor(name, a.shape, mybir.dt.from_np(a.dtype), kind="ExternalInput").ap())
    args.append(nc.dram_tensor("out", arrays["x"].shape, F32, kind="ExternalOutput").ap())
    moe_gnn_kernel(nc, *args)
    return run_bass_kernel_spmd(nc, [arrays], core_ids=[0]).results[0]["out"]
```
